# Optimizing a Trainium2 kernel written in Bass

```python
import numpy as np
import jax
import jax.numpy as jnp

def _softmax(x, axis=-1):
    return jax.nn.softmax(x, axis=axis)

def _gelu(x):
    return jax.nn.gelu(x, approximate=True)

def _silu(x):
    return jax.nn.silu(x)

def _sigmoid(x):
    return jax.nn.sigmoid(x)

def _layernorm(x, axis=-1, eps=1e-05):
    m = jnp.mean(x, axis=axis, keepdims=True)
    v = jnp.var(x, axis=axis, keepdims=True)
    return (x - m) / jnp.sqrt(v + eps)

def _scatter_add(tgt, idx, src, axis=0):
    return tgt.at[idx].add(src)

def _segment_sum(src, seg, n):
    return jax.ops.segment_sum(src, seg, n)
kernel_name = 'mk_adaln_d1_jaxref_r8_26badf'

def setup_inputs(seed: int=0):
    np.random.seed(seed)
    _w = jnp.asarray

    def _L0_attn_setup():
        import jax, jax.numpy as jnp
        import numpy as np
        from math import sqrt
        N_HEAD = 16
        W_SCALE = 0.02

        def _reference_tuple_inner(x, W_dq, W_uq, W_dkv, W_uk, W_uv, W_o):
            B, T, C = x.shape
            nh = N_HEAD
            hs = C // nh
            n_kvl = W_dkv.shape[0]
            k_eff = (W_dq.T @ W_uq.T @ W_uk).reshape(nh, hs, n_kvl)
            v_eff = jnp.transpose((W_uv.T @ W_o.T).reshape(n_kvl, nh, hs), (1, 0, 2))
            c_kv = x @ W_dkv.T
            q = x @ W_dq.T @ W_uq.T
            q = q.reshape(B, T, nh, hs)
            q_lat = jnp.einsum('bqhd,hdl->bhql', q, k_eff)
            attn = jnp.einsum('bhql,bkl->bhqk', q_lat, c_kv) / sqrt(hs)
            causal = jnp.tril(jnp.ones((T, T), dtype=bool))
            attn = jnp.where(causal[None, None], attn, -jnp.inf)
            attn = jax.nn.softmax(attn, axis=-1)
            y_lat = jnp.einsum('bhqk,bkl->bhql', attn, c_kv)
            y = jnp.einsum('bhql,hld->bqhd', y_lat, v_eff).reshape(B, T, C)
            return (y, c_kv)
        key = jax.random.key(seed)
        ks = jax.random.split(key, 7)
        B, T, C = (2, 256, 128)
        QL, KVL = (64, 64)
        return {'x': jax.random.normal(ks[0], (B, T, C), dtype=jnp.float32), 'W_dq': jax.random.normal(ks[1], (QL, C), dtype=jnp.float32) * W_SCALE, 'W_uq': jax.random.normal(ks[2], (C, QL), dtype=jnp.float32) * W_SCALE, 'W_dkv': jax.random.normal(ks[3], (KVL, C), dtype=jnp.float32) * W_SCALE, 'W_uk': jax.random.normal(ks[4], (C, KVL), dtype=jnp.float32) * W_SCALE, 'W_uv': jax.random.normal(ks[5], (C, KVL), dtype=jnp.float32) * W_SCALE, 'W_o': jax.random.normal(ks[6], (C, C), dtype=jnp.float32) * W_SCALE}
    _L0_attn_in = _L0_attn_setup()

    def _L0_ffn_setup():
        import jax, jax.numpy as jnp
        import numpy as np
        from jax import lax
        T, B, I, M, O = (32, 64, 128, 128, 128)

        def _xavier(key, shape):
            fan_out, fan_in = shape
            limit = float(np.sqrt(6.0 / (fan_in + fan_out)))
            return jax.random.uniform(key, shape, jnp.float32, -limit, limit)
        key = jax.random.key(seed)
        ks = jax.random.split(key, 9)
        x = jax.random.normal(ks[0], (T, B, I), jnp.float32)
        return {'x': x, 'wf': _xavier(ks[1], (M, I)), 'uf': _xavier(ks[2], (M, M)), 'bf': jnp.zeros((M,), jnp.float32), 'wi': _xavier(ks[3], (M, I)), 'ui': _xavier(ks[4], (M, M)), 'bi': jnp.zeros((M,), jnp.float32), 'wc': _xavier(ks[5], (M, I)), 'uc': _xavier(ks[6], (M, M)), 'bc': jnp.zeros((M,), jnp.float32), 'wo': _xavier(ks[7], (O, I)), 'uo': _xavier(ks[8], (O, M)), 'bo': jnp.zeros((O,), jnp.float32), 'in_c': jnp.zeros((M,), jnp.float32)}
    _L0_ffn_in = _L0_ffn_setup()
    _L0_c = _w((lambda *s: np.random.randn(*s).astype(np.float32) * 0.05)(8, 128))
    _L0_wmod = _w((lambda *s: np.random.randn(*s).astype(np.float32) * 0.05)(128, 6 * 128) * 128 ** (-0.5))
    _d = {'L0_attn_x': _L0_attn_in['x'], 'L0_attn_W_dq': _L0_attn_in['W_dq'], 'L0_attn_W_uq': _L0_attn_in['W_uq'], 'L0_attn_W_dkv': _L0_attn_in['W_dkv'], 'L0_attn_W_uk': _L0_attn_in['W_uk'], 'L0_attn_W_uv': _L0_attn_in['W_uv'], 'L0_attn_W_o': _L0_attn_in['W_o'], 'L0_ffn_wf': _L0_ffn_in['wf'], 'L0_ffn_uf': _L0_ffn_in['uf'], 'L0_ffn_bf': _L0_ffn_in['bf'], 'L0_ffn_wi': _L0_ffn_in['wi'], 'L0_ffn_ui': _L0_ffn_in['ui'], 'L0_ffn_bi': _L0_ffn_in['bi'], 'L0_ffn_wc': _L0_ffn_in['wc'], 'L0_ffn_uc': _L0_ffn_in['uc'], 'L0_ffn_bc': _L0_ffn_in['bc'], 'L0_ffn_wo': _L0_ffn_in['wo'], 'L0_ffn_uo': _L0_ffn_in['uo'], 'L0_ffn_bo': _L0_ffn_in['bo'], 'L0_ffn_in_c': _L0_ffn_in['in_c'], 'L0_c': _L0_c, 'L0_wmod': _L0_wmod}
    _x0 = _d['L0_attn_x']
    _d['L0_attn_x'] = jax.random.normal(jax.random.fold_in(jax.random.key(seed), 1), (8, 512, 128), dtype=_x0.dtype)
    del _x0
    return _d

def reference(L0_attn_x, L0_attn_W_dq, L0_attn_W_uq, L0_attn_W_dkv, L0_attn_W_uk, L0_attn_W_uv, L0_attn_W_o, L0_ffn_wf, L0_ffn_uf, L0_ffn_bf, L0_ffn_wi, L0_ffn_ui, L0_ffn_bi, L0_ffn_wc, L0_ffn_uc, L0_ffn_bc, L0_ffn_wo, L0_ffn_uo, L0_ffn_bo, L0_ffn_in_c, L0_c, L0_wmod):

    def _L0_attn_ref(x, W_dq, W_uq, W_dkv, W_uk, W_uv, W_o):
        import jax, jax.numpy as jnp
        import numpy as np
        from math import sqrt
        N_HEAD = 16
        W_SCALE = 0.02

        def _reference_tuple_inner(x, W_dq, W_uq, W_dkv, W_uk, W_uv, W_o):
            B, T, C = x.shape
            nh = N_HEAD
            hs = C // nh
            n_kvl = W_dkv.shape[0]
            k_eff = (W_dq.T @ W_uq.T @ W_uk).reshape(nh, hs, n_kvl)
            v_eff = jnp.transpose((W_uv.T @ W_o.T).reshape(n_kvl, nh, hs), (1, 0, 2))
            c_kv = x @ W_dkv.T
            q = x @ W_dq.T @ W_uq.T
            q = q.reshape(B, T, nh, hs)
            q_lat = jnp.einsum('bqhd,hdl->bhql', q, k_eff)
            attn = jnp.einsum('bhql,bkl->bhqk', q_lat, c_kv) / sqrt(hs)
            causal = jnp.tril(jnp.ones((T, T), dtype=bool))
            attn = jnp.where(causal[None, None], attn, -jnp.inf)
            attn = jax.nn.softmax(attn, axis=-1)
            y_lat = jnp.einsum('bhqk,bkl->bhql', attn, c_kv)
            y = jnp.einsum('bhql,hld->bqhd', y_lat, v_eff).reshape(B, T, C)
            return (y, c_kv)
        return _reference_tuple_inner(x, W_dq, W_uq, W_dkv, W_uk, W_uv, W_o)[0]

    def _L0_ffn_ref(x, wf, uf, bf, wi, ui, bi, wc, uc, bc, wo, uo, bo, in_c):
        import jax, jax.numpy as jnp
        import numpy as np
        from jax import lax
        T, B, I, M, O = (32, 64, 128, 128, 128)

        def _xavier(key, shape):
            fan_out, fan_in = shape
            limit = float(np.sqrt(6.0 / (fan_in + fan_out)))
            return jax.random.uniform(key, shape, jnp.float32, -limit, limit)
        batch = x.shape[1]
        c0 = jnp.broadcast_to(in_c, (batch, in_c.shape[0]))

        def step(c, xt):
            ft = jax.nn.sigmoid(xt @ wf.T + c @ uf.T + bf)
            it = jax.nn.sigmoid(xt @ wi.T + c @ ui.T + bi)
            gt = jnp.tanh(xt @ wc.T + c @ uc.T + bc)
            c = ft * c + it * gt
            return (c, None)
        c_final, _ = lax.scan(step, c0, x)
        h = jnp.tanh(jnp.einsum('tbi,oi->tbo', x, wo) + c_final @ uo.T + bo)
        return h
    x = L0_attn_x
    mod = (_silu(L0_c) @ L0_wmod).reshape(L0_c.shape[0], 6, 1, -1)
    sa, ca, ga, sb, cb, gb = (mod[:, 0], mod[:, 1], mod[:, 2], mod[:, 3], mod[:, 4], mod[:, 5])
    ga = (2 * (ga >= 0) - 1) * jnp.maximum(jnp.abs(ga), 0.25)
    gb = (2 * (gb >= 0) - 1) * jnp.maximum(jnp.abs(gb), 0.25)
    h = _layernorm(x, axis=-1) * (1 + ca) + sa
    x = x + ga * _L0_attn_ref(h, L0_attn_W_dq, L0_attn_W_uq, L0_attn_W_dkv, L0_attn_W_uk, L0_attn_W_uv, L0_attn_W_o)
    h = _layernorm(x, axis=-1) * (1 + cb) + sb
    x = x + gb * _L0_ffn_ref(h, L0_ffn_wf, L0_ffn_uf, L0_ffn_bf, L0_ffn_wi, L0_ffn_ui, L0_ffn_bi, L0_ffn_wc, L0_ffn_uc, L0_ffn_bc, L0_ffn_wo, L0_ffn_uo, L0_ffn_bo, L0_ffn_in_c)
    return x

_drawn_inputs = setup_inputs


def setup_inputs(seed=0):
    import zlib

    import numpy as np

    out = dict(_drawn_inputs(seed))
    spreads = {'L0_ffn_bf': (0.0, 0.8),
     'L0_ffn_bi': (0.0, 0.8),
     'L0_ffn_bc': (0.0, 0.639),
     'L0_ffn_bo': (0.0, 0.498),
     'L0_ffn_in_c': (0.0, 0.8)}
    factors = {'L0_attn_W_dq': 8.0,
     'L0_attn_W_uq': 8.0,
     'L0_attn_W_dkv': 8.0,
     'L0_attn_W_uk': 8.0,
     'L0_attn_W_uv': 8.0,
     'L0_attn_W_o': 8.0,
     'L0_ffn_wf': 2.76,
     'L0_ffn_uf': 4.927,
     'L0_ffn_ui': 3.911}
    for name, (base, spread) in spreads.items():
        noise = np.random.default_rng([zlib.crc32(name.encode()), seed]).standard_normal(out[name].shape)
        drawn = base * np.exp(spread * noise) if base else spread * noise
        out[name] = jnp.asarray(drawn.astype(out[name].dtype))
    for name, factor in factors.items():
        out[name] = (out[name] * factor).astype(out[name].dtype)
    return out
```

```python
from contextlib import ExitStack

import numpy as np

import concourse.bass as bass
from concourse import mybir

B, T, C = 8, 512, 128
NH, HS, KVL = 16, 8, 64
NT = T // 128
HG = 4
NG = NH // HG
PARTS = 3
PAIRS_Q = (0, 0, 0, 1, 1, 2)
PAIRS_K = (0, 1, 2, 0, 1, 0)
STACK = len(PAIRS_Q) * HS
MAX_ROW = 120
A_ROWS = 120
A_ITEMS = 10
B_ITEMS = 5
LEAD = 2
SCALE = float(HS) ** -0.5
EPS = 1e-5
MASKED = -1.0e30
LOWEST = -3.0e38

W128 = ["W_uk", "W_uv", "W_oT", "wfT", "wiT", "wcT", "woT", "ufT", "uiT", "ucT", "uoT", "wmod", "cT",
        "bf", "bi", "bc", "in_c"]
WIDTH = dict(W_uk=KVL, W_uv=KVL, wmod=6 * C, cT=B, bf=1, bi=1, bc=1, in_c=1)


def build(nc, x, w64, w128, bo, scratch, out):
    f32, bf16 = mybir.dt.float32, mybir.dt.bfloat16
    ALU, ACT, AX = mybir.AluOpType, mybir.ActivationFunctionType, mybir.AxisListType

    at, n = {}, 0
    for name in W128:
        at[name] = (n, n + WIDTH.get(name, C))
        n = at[name][1]
    w128_cols = n

    with ExitStack() as ctx:
        def sb(name, shape, dt=f32):
            return ctx.enter_context(nc.sbuf_tensor(name, shape, dt))

        def ps(name, shape):
            return ctx.enter_context(nc.psum_tensor(name, shape, f32))

        def sem(name):
            return ctx.enter_context(nc.semaphore(name))

        W64 = sb("W64", [KVL, 3 * C])
        W = sb("W", [128, w128_cols])
        boR = sb("boR", [1, C])
        onesR = sb("onesR", [1, 128])
        ident = sb("ident", [128, 128])
        identb = sb("identb", [128, 128], bf16)
        causal = sb("causal", [128, 128], bf16)
        causalT = sb("causalT", [128, 128], bf16)
        AT = sb("AT", [128, C])
        VE = sb("VE", [KVL, C])
        KE = sb("KE", [KVL, C])
        WQ = sb("WQ", [128, C])
        WK = sb("WK", [128, C])
        WV = sb("WV", [128, C])
        silu_t = sb("silu_t", [128, B])
        silu = sb("silu", [128, B])
        modc = sb("modc", [128, 4, B])
        gate = sb("gate", [128, B, 2, C])
        half_b = sb("half_b", [128, 2])
        expo = sb("expo", [128, NT])
        X = sb("X", [128, B, NT, C])
        ZX = sb("ZX", [128, B, NT, C])
        stat = sb("stat", [128, 2, NT, 6])
        mv = sb("mv", [128, 2, NT, 2])
        varp = sb("varp", [128, 2, NT])
        rstd = sb("rstd", [128, 2, NT])
        xn = sb("xn", [128, 2, NT, C])
        hT = sb("hT", [128, T])
        h2T = sb("h2T", [128, T])
        parts = sb("parts", [128, 2, PARTS, T], bf16)
        rest = sb("rest", [128, 2, T])
        Qs = [sb(f"Qs{i}", [128, NH, T], bf16) for i in range(2)]
        Ks = [sb(f"Ks{i}", [128, NH // 2, T], bf16) for i in range(2)]
        Va = [sb(f"Va{i}", [128, NT, NH, 32]) for i in range(2)]
        bm = sb("bm", [128, 2, HG, NT, 4])
        nm = sb("nm", [128, 2, HG, NT])
        nr = sb("nr", [128, 2, HG, NT])
        nparts = sb("nparts", [128, 2, NT, PARTS, HG], bf16)
        mrow = sb("mrow", [PARTS * HG, 2, T], bf16)
        P = [sb(f"P{i}", [128, 10, T]) for i in range(2)]
        siluB = P[0][:, 0:2, :].rearrange("p a (b q) -> p (a b) q", q=128)
        gsign = P[1][:, 0:4, :].rearrange("p a (b j c) -> p (a b) j c", b=2, j=2)
        gabs = P[1][:, 4:8, :].rearrange("p a (b j c) -> p (a b) j c", b=2, j=2)
        CU = P[1][:, 0, :].rearrange("p (t c) -> p t c", t=NT)
        zt = [P[0][:, i, :].rearrange("p (t c) -> p t c", t=NT) for i in range(2)]
        Y = [sb(f"Y{i}", [128, NG, T]) for i in range(2)]
        rden = sb("rden", [128, NT, NH])
        y = sb("y", [128, NT, C])
        gf = sb("gf", [128, T])
        gi = sb("gi", [128, T])
        gg = sb("gg", [128, T])
        sT = sb("sT", [128, T])

        psA = ps("psA", [128, 2, 512])
        psB = ps("psB", [128, 4, 512])
        psY = ps("psY", [128, 512])
        psM = ps("psM", [128, 512])

        names = """w64_in w128_in bo_in consts setup_mm setup_v th_done silu_done mod_done gate_done
            stat_done rstd_done xn_done var_done h_turned h_copied q_made q_hi q_rest q_mid q_lo k_made k_hi k_rest
            k_mid k_lo v_made v_copied parts_out stacks_in a_ready a_reduced nm_done n_part nr_done n_ready
            m_turned m_copied m_in b_ready exp_done  pv_done y_copied y_turned r_done y_scaled
            ga_done x1_done h2_turned h2_copied f_made i_made g_made f_act i_act g_act u_done v_done s_done
            z_made z_copied cu_made cu_done zsum_done tanh_done zgate_done out_ready out_done""".split()
        S = {k: sem(k) for k in names}
        x_in = [sem(f"x_in{b}") for b in range(B)]
        S["stat2_done"], S["rstd2_done"], S["xn2_done"], S["var2_done"] = (
            sem("stat2_done"), sem("rstd2_done"), sem("xn2_done"), sem("var2_done"))

        block = ctx.enter_context(nc.Block())

        def wait(e, name, value):
            if isinstance(value, int) and value <= 0:
                return
            e.wait_ge(S[name], value)

        def w(name):
            return W[:, at[name][0]:at[name][1]]

        W_dq, W_uqT, W_dkv = (W64[:, i * C:(i + 1) * C] for i in range(3))

        def on_of(s):
            return dict(pre=0 <= s + 2 < B, v=0 <= s + 1 < B, b=0 <= s < B, post=0 <= s - 1 < B,
                        post2=0 <= s - 2 < B,
                        a=[0 <= NG * s + k + LEAD < NG * B for k in range(NG)],
                        m=[0 <= NG * s + k + 1 < NG * B for k in range(NG)])

        def slots(e, job):
            for s in range(-2, B + 2):
                job(s, s % 2, on_of(s))

        def misc_users(s, on):
            order = []

            def use(stage, kind, i, copied, count):
                if stage:
                    order.append(((kind, i), copied, count))

            use(on["post2"], "z", 0, "z_copied", s - 1)
            use(on["m"][0], "m", 0, "m_copied", 4 * s + 2)
            use(on["v"], "v", 0, "v_copied", s + 2)
            use(on["post"], "y", 0, "y_scaled", 4 * (s - 1) + 1)
            use(on["m"][1], "m", 1, "m_copied", 4 * s + 3)
            use(on["post"], "y", 1, "y_scaled", 4 * (s - 1) + 2)
            use(on["post"], "y", 2, "y_scaled", 4 * (s - 1) + 3)
            use(on["post"], "y", 3, "y_scaled", 4 * (s - 1) + 4)
            use(on["pre"], "h", 0, "h_copied", s + 3)
            use(on["m"][2], "m", 2, "m_copied", 4 * s + 4)
            use(on["pre"], "q", 0, "q_rest", s + 3)
            use(on["pre"], "k", 0, "k_rest", s + 3)
            use(on["post"], "h2", 0, "h2_copied", s)
            use(on["post"], "f", 0, "f_act", s)
            use(on["m"][3], "m", 3, "m_copied", 4 * s + 5)
            use(on["post"], "i", 0, "i_act", s)
            use(on["post"], "g", 0, "g_act", s)
            return order

        def misc_free(e, s, on, job):
            order = misc_users(s, on)
            i = [o[0] for o in order].index(job)
            if i:
                wait(e, order[i - 1][1], order[i - 1][2])
                return
            if isinstance(s, int):
                before = s - 1
                while before >= -2 and not misc_users(before, on_of(before)):
                    before -= 1
                if before < -2:
                    return
                last = misc_users(before, on_of(before))[-1]
            else:
                last = misc_users(s - 1, on)[-1]
            wait(e, last[1], last[2])

        @block.sync
        def _(sp):
            sp.dma_start(W64[:, :], w64).then_inc(S["w64_in"], 16)
            for b in range(2):
                sp.dma_start(X[:, b], x[b].rearrange("(t p) c -> p t c", p=128)).then_inc(x_in[b], 16)
            sp.dma_start(boR[:, :], bo).then_inc(S["bo_in"], 16)
            for b in range(2, B):
                sp.dma_start(X[:, b], x[b].rearrange("(t p) c -> p t c", p=128)).then_inc(x_in[b], 16)

            def job(s, par, on):
                for k in range(NG):
                    if k == 0 and on["v"]:
                        wait(sp, "parts_out", 32 * (s + 2))
                        wait(sp, "b_ready", B_ITEMS * NG * s)
                        q_, k_ = Qs[1 - par], Ks[1 - par]
                        for c in range(len(PAIRS_Q)):
                            for e_ in range(2):
                                r = STACK * e_ + HS * c
                                qsrc = scratch[0, PAIRS_Q[c]].rearrange("(g e d) t -> e d g t", e=2, d=HS)[e_]
                                ksrc = scratch[1, PAIRS_K[c]].rearrange("(g e d) t -> e d g t", e=2, d=HS)[e_]
                                sp.dma_start(q_[r:r + HS, e_:NH:2, :], qsrc).then_inc(S["stacks_in"], 16)
                                sp.dma_start(k_[r:r + HS, :, :], ksrc).then_inc(S["stacks_in"], 16)
                    if on["m"][k]:
                        G = 4 * s + k + 1
                        gk = (k + 1) % 4
                        bpar = par if k < 3 else 1 - par
                        wait(sp, "m_copied", G + 1)
                        for p in range(PARTS):
                            sp.dma_start(Qs[bpar][MAX_ROW + p:MAX_ROW + p + 1, gk * HG:(gk + 1) * HG, :],
                                         mrow[p * HG:(p + 1) * HG, (k + 1) % 2, :]).then_inc(S["m_in"], 16)
                    if k == 3 and on["pre"]:
                        wait(sp, "stacks_in", 16 * 24 * (s + 2))
                        for j, lo in enumerate(("q_lo", "k_lo")):
                            wait(sp, lo, s + 3)
                            sp.dma_start(scratch[j].rearrange("a c t -> c a t"), parts[:, j])\
                              .then_inc(S["parts_out"], 16)

            slots(sp, job)
            for b in range(B):
                sp.wait_ge(S["out_ready"], b + 1)
                sp.dma_start(out[b].rearrange("(t p) c -> p t c", p=128), X[:, b]).then_inc(S["out_done"], 16)
            sp.wait_ge(S["out_done"], 16 * B)

        @block.gpsimd
        def _(pool):
            c = S["consts"]
            pool.memset(ident[:, :], 0.0).then_inc(c, 1)
            pool.memset(identb[:, :], 0.0).then_inc(c, 1)
            pool.memset(causal[:, :], 0.0).then_inc(c, 1)
            pool.memset(causalT[:, :], 0.0).then_inc(c, 1)
            pool.memset(expo[:, :], -0.5).then_inc(c, 1)
            pool.memset(onesR[:, :], 1.0).then_inc(c, 1)
            pool.wait_ge(c, 6)
            for m in (ident, identb):
                pool.affine_select(out=m[:, :], in_=m[:, :], compare_op=ALU.not_equal, fill=1.0, base=0,
                                   pattern=[[-1, 128]], channel_multiplier=1).then_inc(c, 1)
            pool.affine_select(out=causal[:, :], in_=causal[:, :], compare_op=ALU.is_ge, fill=MASKED, base=0,
                               pattern=[[-1, 128]], channel_multiplier=1).then_inc(c, 1)
            pool.affine_select(out=causalT[:, :], in_=causalT[:, :], compare_op=ALU.is_ge, fill=MASKED, base=0,
                               pattern=[[1, 128]], channel_multiplier=-1).then_inc(c, 1)
            pool.wait_ge(c, 10)
            for i in range(2):
                pool.memset(Ks[i][96:128, :, :], 1.0).then_inc(c, 1)
            pool.wait_ge(c, 12)
            for i in range(2):
                pool.memset(Qs[i][:, :, :], 0.0).then_inc(c, 1)
            for i in range(2):
                pool.memset(Va[i][:, :, :, :], 0.0).then_inc(c, 1)
            pool.wait_ge(c, 16)
            for i in range(2):
                pool.memset(Va[i][:, :, :, HS:HS + 1], 1.0).then_inc(c, 1)

            def power(j, var, done):
                pool.tensor_tensor(rstd[:, j], varp[:, j], expo[:, :], ALU.pow).then_inc(S[done], 1)

            def low_part(j, name, s):
                wait(pool, name + "_mid", s + 3)
                pool.tensor_tensor(parts[:, j, 2], rest[:, j], parts[:, j, 1], ALU.subtract)\
                    .then_inc(S[name + "_lo"], 1)

            def job(s, par, on):
                b = s - 1

                def gated():
                    wait(pool, "y_scaled", 4 * s)
                    wait(pool, "gate_done", 1)
                    ga = gate[:, b, 0, :].unsqueeze(1).to_broadcast([128, NT, C])
                    pool.tensor_tensor(y[:, :, :], y[:, :, :], ga, ALU.mult).then_inc(S["ga_done"], 1)

                def residual():
                    wait(pool, "ga_done", s)
                    pool.tensor_tensor(X[:, b], X[:, b], y[:, :, :], ALU.add).then_inc(S["x1_done"], 1)

                for k in range(NG):
                    if k == 0 and on["pre"]:
                        wait(pool, "var_done", s + 3)
                        power(0, None, "rstd_done")
                    if k == 2 and on["post"]:
                        gated()
                        residual()
                    if k == 3 and on["pre"]:
                        low_part(0, "q", s)
                    if k == 2 and on["post"]:
                        wait(pool, "var2_done", s)
                        power(1, None, "rstd2_done")
                    if k == 3 and on["pre"]:
                        low_part(1, "k", s)

            slots(pool, job)
            for b in range(B):
                pool.wait_ge(S["tanh_done"], b + 1)
                gb = gate[:, b, 1, :].unsqueeze(1).to_broadcast([128, NT, C])
                pool.tensor_tensor(ZX[:, b], zt[b % 2][:, :, :], gb, ALU.mult).then_inc(S["zgate_done"], 1)

        @block.scalar
        def _(act):
            act.dma_start(W[:, 0:at["wfT"][0]], w128[:, 0:at["wfT"][0]]).then_inc(S["w128_in"], 16)
            act.dma_start(W[:, at["wmod"][0]:], w128[:, at["wmod"][0]:]).then_inc(S["w128_in"], 16)
            act.dma_start(W[:, at["wfT"][0]:at["wmod"][0]], w128[:, at["wfT"][0]:at["wmod"][0]])\
               .then_inc(S["w128_in"], 16)
            act.wait_ge(S["w128_in"], 48)
            act.activation(silu_t[:, :], w("cT"), ACT.Tanh, scale=0.5).then_inc(S["th_done"], 1)

            def turned(dst, made, copied, scale, shift, b, count):
                wait(act, made, count)
                wait(act, "mod_done", 1)
                act.activation(dst[:, :], psM[:, :], ACT.Identity, bias=modc[:, shift, bass.ds(b, 1)],
                               scale=modc[:, scale, bass.ds(b, 1)]).then_inc(S[copied], 1)

            def high_part(j, name, s):
                wait(act, name + "_made", s + 3)
                wait(act, "parts_out", 32 * (s + 2))
                act.activation(parts[:, j, 0], psM[:, :], ACT.Copy).then_inc(S[name + "_hi"], 1)

            def gate_act(dst, name, s, bias, scale):
                wait(act, name + "_made", s)
                wait(act, "s_done", s - 1)
                act.activation(dst[:, :], psM[:, :], ACT.Tanh, bias=bias, scale=scale)\
                   .then_inc(S[name + "_act"], 1)

            def y_copy(G, ypar, gk, b):
                wait(act, "pv_done", G + 1)
                wait(act, "y_turned", 4 * (b - 1))
                act.activation(Y[ypar][:, gk, :], psY[:, :], ACT.Copy).then_inc(S["y_copied"], 1)

            def job(s, par, on):
                for k in range(NG):
                    for i in range(B_ITEMS):
                        if on["b"]:
                            G = 4 * s + k
                            slot = (k + i) % 2
                            wait(act, "b_ready", B_ITEMS * G + i + 1)
                            if i == 0:
                                wait(act, "pv_done", G - 1)
                            act.activation(P[k % 2][:, 2 * i:2 * i + 2, :], psB[:, 2 * slot:2 * slot + 2, :],
                                           ACT.Exp, scale=SCALE).then_inc(S["exp_done"], 1)
                        if i == 0:
                            if k == 0 and on["post"]:
                                y_copy(4 * s - 2, 1 - par, 2, s - 1)
                            if k == 1 and on["post"]:
                                y_copy(4 * s - 1, 1 - par, 3, s - 1)
                            if k > 1 and on["b"]:
                                y_copy(4 * s + k - 2, par, k - 2, s)
                        if i == 2 and on["m"][k]:
                            G = 4 * s + k + 1
                            wait(act, "m_turned", G + 1)
                            wait(act, "m_in", 16 * PARTS * (G - 1))
                            act.activation(mrow[:, (k + 1) % 2, :], psM[0:PARTS * HG, 0:256].bitcast(bf16),
                                           ACT.Copy).then_inc(S["m_copied"], 1)
                        if (k, i) == (0, 0) and on["post2"]:
                            wait(act, "z_made", s - 1)
                            act.activation(ZX[:, s - 2], psM[:, :].rearrange("p (t c) -> p t c", t=NT), ACT.Copy)\
                               .then_inc(S["z_copied"], 1)
                        if (k, i) == (2, 1) and on["pre"]:
                            turned(hT, "h_turned", "h_copied", 1, 0, s + 2, s + 3)
                        if (k, i) == (2, 3) and on["pre"]:
                            high_part(0, "q", s)
                        if (k, i) == (2, 4) and on["pre"]:
                            high_part(1, "k", s)
                        if (k, i) == (3, 0) and on["post"]:
                            turned(h2T, "h2_turned", "h2_copied", 3, 2, s - 1, s)
                        if (k, i) == (3, 1) and on["post"]:
                            gate_act(gf, "f", s, half_b[:, 0:1], 0.5)
                        if (k, i) == (3, 3) and on["post"]:
                            gate_act(gi, "i", s, half_b[:, 1:2], 0.5)
                        if (k, i) == (3, 4) and on["post"]:
                            gate_act(gg, "g", s, w("bc"), 1.0)

            slots(act, job)
            for b in range(B):
                act.wait_ge(S["zsum_done"], b + 1)
                if b >= 2:
                    act.wait_ge(S["zgate_done"], b - 1)
                act.activation(zt[b % 2][:, :, :], ZX[:, b], ACT.Tanh).then_inc(S["tanh_done"], 1)

        @block.vector
        def _(dve):
            sv = [0]

            def done_setup(ins):
                sv[0] += 1
                ins.then_inc(S["setup_v"], 1)
                return sv[0]

            for G2 in range(2):
                dve.memset(bm[:, G2], LOWEST).then_inc(S["setup_v"], 1)
            dve.memset(sT[:, :], 0.0).then_inc(S["setup_v"], 1)
            sv[0] = 3
            dve.wait_ge(S["setup_mm"], 1)
            done_setup(dve.tensor_copy(WQ[:, :], psB[:, 0, 0:C]))
            done_setup(dve.tensor_copy(AT[:, :], psB[:, 1, 0:C]))
            done_setup(dve.tensor_copy(VE[:, :], psB[0:KVL, 2, 0:C]))
            dve.wait_ge(S["w128_in"], 48)
            dve.wait_ge(S["th_done"], 1)
            done_setup(dve.scalar_tensor_tensor(out=silu[:, :], in0=silu_t[:, :], scalar=1.0, in1=w("cT"),
                                                op0=ALU.add, op1=ALU.mult))
            done_setup(dve.tensor_scalar(half_b[:, :], W[:, at["bf"][0]:at["bi"][1]], 0.5, None, ALU.mult))
            u4 = W[:, at["ufT"][0]:at["uoT"][1]]
            done_setup(dve.tensor_scalar(u4, u4, 0.5, None, ALU.mult))
            dve.wait_ge(S["setup_v"], 9)
            done_setup(dve.tensor_scalar(sT[:, :], sT[:, :], w("in_c"), 2.0, ALU.add, ALU.mult))
            done_setup(dve.tensor_scalar(siluB[:, :, :], silu[:, :].unsqueeze(2).to_broadcast([128, B, 128]),
                                         0.5, None, ALU.mult))
            dve.wait_ge(S["setup_mm"], 2)
            done_setup(dve.tensor_copy(KE[:, :], psB[0:KVL, 0, 0:C]))
            done_setup(dve.tensor_copy(WV[:, :], psB[:, 1, 0:C]))
            dve.wait_ge(S["setup_mm"], 3)
            done_setup(dve.tensor_copy(WK[:, :], psB[:, 2, 0:C]))
            mps = psA[:, 0, 0:4 * B].rearrange("p (j b) -> p j b", j=4)
            done_setup(dve.tensor_scalar(modc[:, 0:4:2], mps[:, 0:4:2], 0.0, None, ALU.add))
            dve.tensor_scalar(modc[:, 1:4:2], mps[:, 1:4:2], 1.0, None, ALU.add).then_inc(S["mod_done"], 1)
            sv_before_gate = sv[0]

            def gates():
                dve.wait_ge(S["setup_mm"], 4)
                gp = psB[:, :, :].rearrange("p k (a j c) -> p (k a) j c", a=2, j=2)
                n1 = done_setup(dve.tensor_copy(gabs[:, :, :, :], gp))
                dve.wait_ge(S["setup_v"], n1)
                done_setup(dve.tensor_scalar(gsign[:, :, :, :], gabs[:, :, :, :], 0.0, 2.0, ALU.is_ge, ALU.mult))
                n2 = done_setup(dve.scalar_tensor_tensor(out=gate[:, :, :, :], in0=gabs[:, :, :, :], scalar=-1.0,
                                                         in1=gabs[:, :, :, :], op0=ALU.mult, op1=ALU.max))
                dve.wait_ge(S["setup_v"], n2)
                n2 = done_setup(dve.tensor_scalar(gate[:, :, :, :], gate[:, :, :, :], 0.25, None, ALU.max))
                dve.wait_ge(S["setup_v"], n2)
                dve.scalar_tensor_tensor(out=gate[:, :, :, :], in0=gsign[:, :, :, :], scalar=-1.0,
                                         in1=gate[:, :, :, :], op0=ALU.add, op1=ALU.mult)\
                   .then_inc(S["gate_done"], 1)

            gates()

            def norm_stats(j, b, two, count):
                if not two and isinstance(b, int):
                    dve.wait_ge(x_in[b], 16)
                for t in range(NT):
                    last = dve.bn_stats(stat[:, j, t, :], X[:, b, t, :])
                last.then_inc(S[f"stat{two}_done"], 1)
                wait(dve, f"stat{two}_done", count)
                for t in range(NT):
                    last = dve.bn_aggr(mv[:, j, t, :], stat[:, j, t, :])
                last.then_inc(S[f"stat{two}_done"], 1)
                return

            def norm_var(j, two, count):
                wait(dve, f"stat{two}_done", 2 * count)
                dve.tensor_scalar(varp[:, j], mv[:, j, :, 1], EPS, None, ALU.add).then_inc(S[f"var{two}_done"], 1)

            def norm_apply(j, b, two, count):
                wait(dve, f"rstd{two}_done", count)
                for t in range(NT):
                    last = dve.tensor_scalar(xn[:, j, t], X[:, b, t, :], mv[:, j, t, 0:1], rstd[:, j, t:t + 1],
                                             ALU.subtract, ALU.mult)
                last.then_inc(S[f"xn{two}_done"], 1)

            def rest_parts(j, name, s):
                wait(dve, name + "_hi", s + 3)
                dve.tensor_tensor(rest[:, j], psM[:, :], parts[:, j, 0], ALU.subtract)\
                   .then_inc(S[name + "_rest"], 1)
                wait(dve, name + "_rest", s + 3)
                dve.tensor_copy(parts[:, j, 1], rest[:, j]).then_inc(S[name + "_mid"], 1)

            def reduce_item(G, kk, i):
                wait(dve, "a_ready", A_ITEMS * G + i + 1)
                bank = psA[:, i % 2, :].rearrange("p (n c) -> p n c", n=4)
                d = bm[:, kk % 2]
                if i < 4:
                    o = d[:, i, 3, :]
                elif i < 8:
                    o = d[:, i - 4].rearrange("p a b -> p (a b)")[:, 1:5]
                else:
                    o = d[:, 2 * (i - 8):2 * (i - 8) + 2, 2, 0:2]
                dve.tensor_reduce(o, bank, AX.X, ALU.max).then_inc(S["a_reduced"], 1)

            def finish_max(G, kk):
                wait(dve, "a_reduced", A_ITEMS * (G + 1))
                dve.tensor_reduce(nm[:, kk % 2], bm[:, kk % 2], AX.X, ALU.max, negate=True)\
                   .then_inc(S["nm_done"], 1)

            def part1(G, kk):
                wait(dve, "nm_done", G + 1)
                wait(dve, "m_turned", G - 1)
                dve.tensor_copy(nparts[:, kk % 2, :, 0, :], nm[:, kk % 2].rearrange("p h t -> p t h"))\
                   .then_inc(S["n_part"], 1)

            def part1r(G, kk):
                wait(dve, "n_part", 2 * G + 1)
                dve.tensor_tensor(nr[:, kk % 2], nm[:, kk % 2],
                                  nparts[:, kk % 2, :, 0, :].rearrange("p t h -> p h t"), ALU.subtract)\
                   .then_inc(S["nr_done"], 1)

            def part2(G, kk):
                wait(dve, "nr_done", G + 1)
                dve.tensor_copy(nparts[:, kk % 2, :, 1, :], nr[:, kk % 2].rearrange("p h t -> p t h"))\
                   .then_inc(S["n_part"], 1)

            def part3(G, kk):
                wait(dve, "n_part", 2 * G + 2)
                dve.tensor_tensor(nparts[:, kk % 2, :, 2, :], nr[:, kk % 2].rearrange("p h t -> p t h"),
                                  nparts[:, kk % 2, :, 1, :], ALU.subtract).then_inc(S["n_ready"], 1)

            small = [finish_max, part1, part1r, part2, part3]

            def scale_y(t, b):
                wait(dve, "y_turned", 4 * b + t + 1)
                t_ = psM[:, :].rearrange("p (h d) -> p h d", d=32)
                dve.reciprocal(rden[:, t], t_[:, :, HS]).then_inc(S["r_done"], 1)
                wait(dve, "r_done", 4 * b + t + 1)
                if t == 0:
                    wait(dve, "x1_done", b)
                dve.tensor_tensor(y[:, t].rearrange("p (h d) -> p h d", d=HS), t_[:, :, 0:HS],
                                  rden[:, t].unsqueeze(2).to_broadcast([128, NH, HS]), ALU.mult)\
                   .then_inc(S["y_scaled"], 1)

            def job(s, par, on):
                for k in range(NG):
                    for i in range(A_ITEMS):
                        if on["a"][k]:
                            reduce_item(4 * s + k + LEAD, k, i)
                        G1 = 4 * s + k + LEAD - 1
                        prev = on["m"][k]
                        if i < 5 and prev:
                            small[i](G1, k + 1)
                        if (k, i) == (0, 1) and on["post2"]:
                            wait(dve, "g_act", s - 1)
                            wait(dve, "i_act", s - 1)
                            dve.scalar_tensor_tensor(out=gi[:, :], in0=gi[:, :], scalar=1.0, in1=gg[:, :],
                                                     op0=ALU.add, op1=ALU.mult).then_inc(S["v_done"], 1)
                        if (k, i) == (0, 2) and on["post2"]:
                            wait(dve, "v_done", s - 1)
                            wait(dve, "u_done", s - 1)
                            dve.scalar_tensor_tensor(out=sT[:, :], in0=gf[:, :], scalar=0.5, in1=gi[:, :],
                                                     op0=ALU.mult, op1=ALU.add).then_inc(S["s_done"], 1)
                        if (k, i) == (0, 3) and on["pre"]:
                            norm_stats(0, s + 2, "", 2 * (s + 2) + 1)
                        if (k, i) == (0, 4) and on["pre"]:
                            norm_var(0, "", s + 3)
                        if (k, i) == (0, 9) and on["pre"]:
                            norm_apply(0, s + 2, "", s + 3)
                        if (k, i) == (1, 1) and on["v"]:
                            wait(dve, "v_made", s + 2)
                            wait(dve, "pv_done", 4 * s)
                            if isinstance(s, int) and s < 1:
                                dve.wait_ge(S["consts"], 18)
                            dve.tensor_copy(Va[1 - par][:, :, :, 0:HS],
                                            psM[:, :].rearrange("p (t h d) -> p t h d", t=NT, d=HS))\
                               .then_inc(S["v_copied"], 1)
                        if on["post"] and (k, i) in ((1, 3), (1, 7), (1, 9), (2, 1)):
                            scale_y(((1, 3), (1, 7), (1, 9), (2, 1)).index((k, i)), s - 1)
                        if (k, i) == (2, 5) and on["post"]:
                            wait(dve, "x1_done", s)
                            norm_stats(1, s - 1, "2", 2 * (s - 1) + 1)
                        if (k, i) == (2, 6) and on["post"]:
                            norm_var(1, "2", s)
                        if (k, i) == (2, 8) and on["pre"]:
                            rest_parts(0, "q", s)
                        if (k, i) == (2, 9):
                            if on["post"]:
                                norm_apply(1, s - 1, "2", s)
                            if on["pre"]:
                                rest_parts(1, "k", s)
                        if (k, i) == (3, 5) and on["post"]:
                            wait(dve, "f_act", s)
                            dve.scalar_tensor_tensor(out=gf[:, :], in0=gf[:, :], scalar=1.0, in1=sT[:, :],
                                                     op0=ALU.add, op1=ALU.mult).then_inc(S["u_done"], 1)

            slots(dve, job)
            dve.wait_ge(S["cu_made"], 1)
            dve.tensor_copy(CU[:, :, :], psA[:, 0, :].rearrange("p (t c) -> p t c", t=NT)).then_inc(S["cu_done"], 1)
            dve.wait_ge(S["cu_done"], 1)

            def add_state(b):
                if b == 0:
                    dve.wait_ge(S["z_copied"], B)
                dve.tensor_tensor(ZX[:, b], ZX[:, b], CU[:, :, :], ALU.add).then_inc(S["zsum_done"], 1)

            for b in range(B + 2):
                if b < B:
                    add_state(b)
                if b >= 2:
                    dve.wait_ge(S["zgate_done"], b - 1)
                    dve.tensor_tensor(X[:, b - 2], X[:, b - 2], ZX[:, b - 2], ALU.add)\
                       .then_inc(S["out_ready"], 1)

        @block.tensor
        def _(pe):
            def mm(o, l, r, start=True, stop=True):
                return pe.matmul(o, l, r, start=start, stop=stop)

            pe.wait_ge(S["w64_in"], 16)
            pe.wait_ge(S["w128_in"], 48)
            mm(psB[:, 0, 0:C], W_dq, W_uqT)
            mm(psB[:, 1, 0:C], W_uqT, W_dq)
            mm(psB[0:KVL, 2, 0:C], w("W_uv"), w("W_oT")).then_inc(S["setup_mm"], 1)
            pe.wait_ge(S["setup_v"], 6)
            mm(psB[0:KVL, 0, 0:C], w("W_uk"), AT[:, :])
            mm(psB[:, 1, 0:C], W_dkv, VE[:, :]).then_inc(S["setup_mm"], 1)
            pe.wait_ge(S["setup_v"], 13)
            mm(psB[:, 2, 0:C], W_dkv, KE[:, :])
            wm = w("wmod").rearrange("p (j c) -> p j c", j=6)
            for n_, j in enumerate((0, 1, 3, 4)):
                last = mm(psA[:, 0, n_ * B:(n_ + 1) * B], wm[:, j], siluB[:, :, 0])
            last.then_inc(S["setup_mm"], 1)
            pe.wait_ge(S["setup_v"], 14)
            for b in range(B):
                o = psB[:, b // 2, (b % 2) * 256:(b % 2) * 256 + 256].rearrange("p (j c) -> p j c", j=2)
                last = mm(o, siluB[:, b, :], wm[:, 2:6:3, :])
            last.then_inc(S["setup_mm"], 1)
            pe.wait_ge(S["consts"], 18)
            pe.wait_ge(S["mod_done"], 1)
            pe.wait_ge(S["gate_done"], 1)

            def scores_max(G, gk, bpar, i):
                wait(pe, "a_reduced", A_ITEMS * G + i - 1)
                q_, k_ = Qs[bpar], Ks[bpar]
                bank = psA[:, i % 2, :]

                def tile(h, t, c0):
                    n_ = (t + 1) * 128
                    hh = gk * HG + h
                    mm(bank[:, c0:c0 + n_], q_[0:A_ROWS, hh, t * 128:(t + 1) * 128], k_[0:A_ROWS, hh // 2, 0:n_],
                       True, False)
                    return mm(bank[:, c0 + n_ - 128:c0 + n_], identb[:, :], causal[:, :], False, True)

                if i < 4:
                    last = tile(i, 3, 0)
                elif i < 8:
                    tile(i - 4, 2, 0)
                    last = tile(i - 4, 0, 384)
                else:
                    tile(2 * (i - 8), 1, 0)
                    last = tile(2 * (i - 8) + 1, 1, 256)
                last.then_inc(S["a_ready"], 1)

            def scores(G, k, bpar, i):
                wait(pe, "exp_done", B_ITEMS * G + i - 1)
                q_, k_ = Qs[bpar], Ks[bpar]
                slot = (k + i) % 2

                def tile(h, kb, bank, c0):
                    hh = k * HG + h
                    mm(psB[:, 2 * slot + bank, c0:c0 + T - kb * 128],
                       k_[:, hh // 2, kb * 128:(kb + 1) * 128], q_[:, hh, kb * 128:T], True, False)
                    return mm(psB[:, 2 * slot + bank, c0:c0 + 128], identb[:, :], causalT[:, :], False, True)

                for bank in range(2):
                    if i < 2:
                        last = tile(2 * i + bank, 0, bank, 0)
                    elif i < 4:
                        h = 2 * (i - 2) + bank
                        tile(h, 1, bank, 0)
                        last = tile(h, 3, bank, 384)
                    else:
                        tile(2 * bank, 2, bank, 0)
                        last = tile(2 * bank + 1, 2, bank, 256)
                last.then_inc(S["b_ready"], 1)

            def p_view(p_, h, kb):
                if kb == 0:
                    return p_[:, h, 0:512]
                if kb == 1:
                    return p_[:, 4 + h, 0:384]
                if kb == 3:
                    return p_[:, 4 + h, 384:512]
                return p_[:, 8 + h // 2, (h % 2) * 256:(h % 2) * 256 + 256]

            def values(G, gk, bpar, kb):
                if kb == 0:
                    wait(pe, "exp_done", B_ITEMS * (G + 1))
                    wait(pe, "y_copied", G)
                for h in range(HG):
                    last = mm(psY[32 * h:32 * h + 32, kb * 128:T], Va[bpar][:, kb, gk * HG + h, :],
                              p_view(P[gk % 2], h, kb), kb == 0, kb == NT - 1)
                if kb == NT - 1:
                    last.then_inc(S["pv_done"], 1)

            def job(s, par, on):
                def max_rows(k):
                    G = 4 * s + k + 1
                    misc_free(pe, s, on, ("m", k))
                    wait(pe, "n_ready", G + 1)
                    for seg, t in enumerate((2, 0, 1, 3)):
                        o = psM[0:PARTS * HG, t * 64:(t + 1) * 64].bitcast(bf16)
                        last = pe.transpose(o, nparts[:, (k + 1) % 2, seg].rearrange("p a h -> p (a h)"),
                                            identb[:, :])
                    last.then_inc(S["m_turned"], 1)

                def turn(dst_j, name, ready, count, jb):
                    misc_free(pe, s, on, jb)
                    wait(pe, ready, count)
                    for t in range(NT):
                        last = pe.transpose(psM[:, t * 128:(t + 1) * 128], xn[:, dst_j, t], ident[:, :])
                    last.then_inc(S[name], 1)

                def project(weight, name, jb, count):
                    misc_free(pe, s, on, jb)
                    wait(pe, "h_copied", count)
                    mm(psM[:, :], weight, hT[:, :]).then_inc(S[name], 1)

                def turn_y(t):
                    misc_free(pe, s, on, ("y", t))
                    wait(pe, "y_copied", 4 * s)
                    for g in range(NG):
                        last = pe.transpose(psM[:, g * 128:(g + 1) * 128],
                                            Y[1 - par][:, g, t * 128:(t + 1) * 128], ident[:, :])
                    last.then_inc(S["y_turned"], 1)

                def gate_mm(wx, wh, name, jb):
                    misc_free(pe, s, on, jb)
                    wait(pe, "h2_copied", s)
                    mm(psM[:, :], w(wx), h2T[:, :], True, False)
                    wait(pe, "s_done", s - 1)
                    mm(psM[:, :], w(wh), sT[:, :], False, True).then_inc(S[name], 1)

                for k in range(NG):
                    for i in range(B_ITEMS):
                        if on["b"]:
                            if k == 0 and i == 0:
                                pass
                            if i == 0:
                                wait(pe, "m_in", 16 * PARTS * (4 * s + k + 1))
                            scores(4 * s + k, k, par, i)
                        if on["a"][k]:
                            G = 4 * s + k + LEAD
                            if k == 2 and i == 0:
                                wait(pe, "stacks_in", 16 * 24 * (s + 2))
                            for a in range(2):
                                scores_max(G, (k + LEAD) % 4, par if k < 2 else 1 - par, 2 * i + a)
                        if i > 0:
                            if k == 0 and on["post"]:
                                values(4 * s - 1, 3, 1 - par, i - 1)
                            if k > 0 and on["b"]:
                                values(4 * s + k - 1, k - 1, par, i - 1)
                        if (k, i) == (0, 0) and on["post2"]:
                            misc_free(pe, s, on, ("z", 0))
                            for t in range(NT):
                                last = mm(psM[:, t * 128:(t + 1) * 128], h2T[:, t * 128:(t + 1) * 128], w("woT"))
                            last.then_inc(S["z_made"], 1)
                        if (k, i) == (1, 0) and on["v"]:
                            misc_free(pe, s, on, ("v", 0))
                            wait(pe, "h_copied", s + 2)
                            for t in range(NT):
                                last = mm(psM[:, t * 128:(t + 1) * 128], hT[:, t * 128:(t + 1) * 128], WV[:, :])
                            last.then_inc(S["v_made"], 1)
                        if i == 2 and on["m"][k]:
                            max_rows(k)
                        if on["post"] and (k, i) in ((1, 1), (1, 3), (1, 4), (2, 0)):
                            turn_y(((1, 1), (1, 3), (1, 4), (2, 0)).index((k, i)))
                        if (k, i) == (2, 1) and on["pre"]:
                            turn(0, "h_turned", "xn_done", s + 3, ("h", 0))
                        if (k, i) == (2, 3) and on["pre"]:
                            project(WQ[:, :], "q_made", ("q", 0), s + 3)
                        if (k, i) == (2, 4) and on["pre"]:
                            project(WK[:, :], "k_made", ("k", 0), s + 3)
                        if (k, i) == (3, 0) and on["post"]:
                            turn(1, "h2_turned", "xn2_done", s, ("h2", 0))
                        if (k, i) == (3, 1) and on["post"]:
                            gate_mm("wfT", "ufT", "f_made", ("f", 0))
                        if (k, i) == (3, 3) and on["post"]:
                            gate_mm("wiT", "uiT", "i_made", ("i", 0))
                        if (k, i) == (3, 4) and on["post"]:
                            gate_mm("wcT", "ucT", "g_made", ("g", 0))

            slots(pe, job)
            pe.wait_ge(S["s_done"], B)
            pe.wait_ge(S["bo_in"], 16)
            pe.wait_ge(S["a_reduced"], A_ITEMS * NG * B)
            for t in range(NT):
                o = psA[:, 0, t * 128:(t + 1) * 128]
                mm(o, sT[:, t * 128:(t + 1) * 128], w("uoT"), True, False)
                last = mm(o, onesR[:, :], boR[:, :], False, True)
            last.then_inc(S["cu_made"], 1)


def kernel(**inputs):
    import concourse.bacc as bacc
    from concourse.bass_utils import run_bass_kernel_spmd

    a = {k.replace("L0_", "").replace("attn_", "").replace("ffn_", ""): np.asarray(v) for k, v in inputs.items()}
    col = {"W_uk": a["W_uk"], "W_uv": a["W_uv"], "W_oT": a["W_o"].T, "wmod": a["wmod"], "cT": a["c"].T}
    for n in ("wf", "wi", "wc", "wo", "uf", "ui", "uc", "uo"):
        col[n + "T"] = a[n].T
    for n in ("bf", "bi", "bc", "in_c"):
        col[n] = a[n][:, None]
    arrays = {
        "x": np.ascontiguousarray(a["x"]),
        "w64": np.ascontiguousarray(np.concatenate([a["W_dq"], a["W_uq"].T, a["W_dkv"]], axis=1)),
        "w128": np.ascontiguousarray(np.concatenate([col[n] for n in W128], axis=1)),
        "bo": np.ascontiguousarray(a["bo"][None, :]),
    }
    nc = bacc.Bacc("TRN2", target_bir_lowering=False, num_devices=1)
    f32 = mybir.dt.float32
    aps = [nc.dram_tensor(k, v.shape, f32, kind="ExternalInput").ap() for k, v in arrays.items()]
    scratch = nc.dram_tensor("scratch", [2, PARTS, C, T], mybir.dt.bfloat16, kind="Internal").ap()
    out = nc.dram_tensor("out", [B, T, C], f32, kind="ExternalOutput").ap()
    build(nc, *aps, scratch, out)
    r = run_bass_kernel_spmd(nc, [arrays], core_ids=[0])
    return r.results[0]["out"]
```

```python
from contextlib import ExitStack

import numpy as np

import concourse.bass as bass
from concourse import mybir

B, T, C = 8, 512, 128
NH, HS, KVL = 16, 8, 64
NT = T // 128
HG = 4
NG = NH // HG
PARTS = 3
PAIRS = ((0, 0), (0, 1), (0, 2), (1, 0), (1, 1), (2, 0))
STACK = len(PAIRS) * HS
MAX_ROW = 2 * STACK
A_ITEMS = 10
RUNS = ((0, 3, 0), (3, 2, 1), (5, 1, 2))
LOADS = 16 * 12
B_ITEMS = 5
LEAD = 2
SCALE = float(HS) ** -0.5
EPS = 1e-5
MASKED = -1.0e30
LOWEST = -3.0e38
ONE_BF16 = np.uint16(0x3F80)

W128 = ["W_uk", "W_uv", "W_oT", "wfT", "wiT", "wcT", "woT", "ufT", "uiT", "ucT", "uoT", "wmod", "cT",
        "bf", "bi", "bc", "in_c"]
WIDTH = dict(W_uk=KVL, W_uv=KVL, wmod=6 * C, cT=B, bf=1, bi=1, bc=1, in_c=1)


def build(nc, x, w64, w128, bo, sel, scratch, out):
    f32, bf16 = mybir.dt.float32, mybir.dt.bfloat16
    ALU, ACT, AX = mybir.AluOpType, mybir.ActivationFunctionType, mybir.AxisListType

    at, n = {}, 0
    for name in W128:
        at[name] = (n, n + WIDTH.get(name, C))
        n = at[name][1]
    w128_cols = n

    with ExitStack() as ctx:
        def sb(name, shape, dt=f32):
            return ctx.enter_context(nc.sbuf_tensor(name, shape, dt))

        def ps(name, shape):
            return ctx.enter_context(nc.psum_tensor(name, shape, f32))

        def sem(name):
            return ctx.enter_context(nc.semaphore(name))

        W64 = sb("W64", [KVL, 3 * C])
        W = sb("W", [128, w128_cols])
        boR = sb("boR", [1, C])
        onesR = sb("onesR", [1, 128])
        ident = sb("ident", [128, 128])
        identb = sb("identb", [128, 128], bf16)
        causal = sb("causal", [128, 128], bf16)
        causalT = sb("causalT", [128, 128], bf16)
        AT = sb("AT", [128, C])
        VE = sb("VE", [KVL, C])
        KE = sb("KE", [KVL, C])
        WQ = sb("WQ", [128, C])
        WK = sb("WK", [128, C])
        WV = sb("WV", [128, C])
        silu_t = sb("silu_t", [128, B])
        silu = sb("silu", [128, B])
        modc = sb("modc", [128, 4, B])
        gcol = sb("gcol", [128, 2, B])
        gsign = sb("gsign", [128, 2, B])
        gabs = sb("gabs", [128, 2, B])
        gate = sb("gate", [128, B, 2, C])
        half_b = sb("half_b", [128, 2])
        expo = sb("expo", [128, NT])
        X = sb("X", [128, B, NT, C])
        ZX = sb("ZX", [128, B, NT, C])
        stat = sb("stat", [128, 2, NT, 6])
        mv = sb("mv", [128, 2, NT, 2])
        varp = sb("varp", [128, 2, NT])
        rstd = sb("rstd", [128, 2, NT])
        xn = sb("xn", [128, 2, NT, C])
        hT = sb("hT", [128, T])
        h2T = sb("h2T", [128, T])
        parts = sb("parts", [128, 2, PARTS, T], bf16)
        rest = sb("rest", [128, 2, T])
        Qs = [sb(f"Qs{i}", [128, NH // 2, T], bf16) for i in range(2)]
        Ks = [sb(f"Ks{i}", [128, NH, T], bf16) for i in range(2)]
        Va = [sb(f"Va{i}", [128, NT, NH, 32]) for i in range(2)]
        bm = sb("bm", [128, 2, HG, NT, 4])
        nm = sb("nm", [128, 2, HG, NT])
        nr = sb("nr", [128, 2, HG, NT])
        nparts = sb("nparts", [128, 2, NT, PARTS, HG], bf16)
        P = [sb(f"P{i}", [128, 10, T]) for i in range(2)]
        zt = [P[0][:, i, :].rearrange("p (t c) -> p t c", t=NT) for i in range(B)]
        Y = [sb(f"Y{i}", [128, NG, T]) for i in range(2)]
        rden = sb("rden", [128, NT, NH])
        y = sb("y", [128, NT, C])
        gf = sb("gf", [128, T])
        gi = sb("gi", [128, T])
        gg = sb("gg", [128, T])
        sT = sb("sT", [128, T])

        psA = ps("psA", [128, 2, 512])
        psB = ps("psB", [128, 4, 512])
        psY = ps("psY", [128, 512])
        psM = ps("psM", [128, 512])

        names = """gate_made w64_in w128_in bo_in consts setup_mm setup_v th_done silu_done mod_made state_set mod_done gate_done
            stat_done rstd_done xn_done var_done h_turned h_copied q_made q_hi q_rest q_mid q_lo k_made k_hi k_rest
            k_mid k_lo v_made v_copied stacks_in a_ready a_reduced nm_done n_part nr_done n_ready
            m_turned m_copied q_zero ks0_zero ks1_zero va_zero gcol_done sel_in w_a w_mod w_rest b_ready exp_done  pv_done y_copied y_turned r_done y_scaled
            ga_done x1_done h2_turned h2_copied f_made i_made g_made f_act i_act g_act u_done v_done s_done
            z_made z_copied cu_made cu_done zsum_done tanh_done zgate_pool zgate_done odd_ready even_ready out_done""".split()
        S = {k: sem(k) for k in names}
        x_in = [sem(f"x_in{b}") for b in range(B)]
        part_out = [[sem(f"{name}{p}_out") for p in range(PARTS)] for name in "qk"]
        S["stat2_done"], S["rstd2_done"], S["xn2_done"], S["var2_done"] = (
            sem("stat2_done"), sem("rstd2_done"), sem("xn2_done"), sem("var2_done"))

        block = ctx.enter_context(nc.Block())

        def wait(e, name, value):
            if isinstance(value, int) and value <= 0:
                return
            e.wait_ge(S[name], value)

        def key_at(h):
            return (h % 2) * (NH // 2) + h // 2

        def w(name):
            return W[:, at[name][0]:at[name][1]]

        W_dq, W_uqT, W_dkv = (W64[:, i * C:(i + 1) * C] for i in range(3))

        def on_of(s):
            return dict(pre=0 <= s + 2 < B, v=0 <= s + 1 < B, b=0 <= s < B, post=0 <= s - 1 < B,
                        post2=0 <= s - 2 < B,
                        a=[0 <= NG * s + k + LEAD < NG * B for k in range(NG)],
                        m=[0 <= NG * s + k + 1 < NG * B for k in range(NG)])

        def slots(e, job):
            for s in range(-1, B + 2):
                job(s, s % 2, on_of(s))

        def misc_users(s, on):
            order = []
            if isinstance(s, int) and s == -2:
                return [(("h", 0), "h_copied", 1)]

            def use(stage, kind, i, copied, count):
                if stage:
                    order.append(((kind, i), copied, count))

            use(on["post2"], "z", 0, "z_copied", s - 1)
            use(on["m"][0], "m", 0, "m_copied", 4 * s + 2)
            use(on["v"], "v", 0, "v_copied", s + 2)
            use(on["post"], "y", 0, "y_scaled", 4 * (s - 1) + 1)
            use(on["m"][1], "m", 1, "m_copied", 4 * s + 3)
            use(on["post"], "y", 1, "y_scaled", 4 * (s - 1) + 2)
            use(on["post"], "y", 2, "y_scaled", 4 * (s - 1) + 3)
            use(on["post"], "y", 3, "y_scaled", 4 * (s - 1) + 4)
            use(on["pre"], "h", 0, "h_copied", s + 3)
            use(on["m"][2], "m", 2, "m_copied", 4 * s + 4)
            use(on["pre"], "q", 0, "q_rest", s + 3)
            use(on["pre"], "k", 0, "k_rest", s + 3)
            use(on["post"], "h2", 0, "h2_copied", s)
            use(on["post"], "f", 0, "f_act", s)
            use(on["m"][3], "m", 3, "m_copied", 4 * s + 5)
            use(on["post"], "i", 0, "i_act", s)
            use(on["post"], "g", 0, "g_act", s)
            return order

        LAST_BANKS = {
            B: {("y", t): (psB[:, t, :], ("exp_done", B_ITEMS * NG * B)) for t in range(NT)},
            B + 1: {("z", 0): (psB[:, 0, :], ("y_scaled", NT * B))},
        }
        LAST_BANKS[B][("f", 0)] = (psA[:, 0, :], ("a_reduced", A_ITEMS * NG * B))
        LAST_BANKS[B][("i", 0)] = (psA[:, 1, :], ("a_reduced", A_ITEMS * NG * B))
        LAST_BANKS[B][("g", 0)] = (psY[:, :], ("y_copied", NG * B))
        LAST_BANKS[B][("h2", 0)] = (psM[:, :], ("z_copied", B - 1))

        def bank_of(s, kind, i=0):
            if isinstance(s, int) and (kind, i) in LAST_BANKS.get(s, {}):
                return LAST_BANKS[s][kind, i][0]
            return psM[:, :]

        def misc_free(e, s, on, job):
            if isinstance(s, int) and job in LAST_BANKS.get(s, {}):
                wait(e, *LAST_BANKS[s][job][1])
                return
            order = misc_users(s, on)
            i = [o[0] for o in order].index(job)
            if i:
                wait(e, order[i - 1][1], order[i - 1][2])
                return
            if isinstance(s, int):
                before = s - 1
                while before >= -2 and not misc_users(before, on_of(before)):
                    before -= 1
                if before < -2:
                    return
                last = misc_users(before, on_of(before))[-1]
            else:
                last = misc_users(s - 1, on)[-1]
            wait(e, last[1], last[2])

        @block.sync
        def _(sp):
            def store_parts(s):
                wait(sp, "stacks_in", LOADS * (s + 2))
                for j, name in enumerate("qk"):
                    for p in range(PARTS):
                        wait(sp, name + ("_hi", "_mid", "_lo")[p], s + 3)
                        sp.dma_start(scratch[j, p].rearrange("e d g t -> g (e d) t"), parts[:, j, p])\
                          .then_inc(part_out[j][p], 16)

            def load_stacks(s):
                wait(sp, "b_ready", B_ITEMS * NG * s)
                if s < 1:
                    wait(sp, "q_zero", s + 2)
                    wait(sp, "ks0_zero" if s < 0 else "ks1_zero", 1)
                q_, k_ = Qs[(s + 1) % 2], Ks[(s + 1) % 2]
                for e in range(2):
                    for first, n, part in RUNS:
                        if e == 0:
                            sp.wait_ge(part_out[0][part], 16 * (s + 2))
                        r = STACK * e + HS * first
                        src = scratch[0, part:part + 1, e].rearrange("p d g t -> p d (g t)")
                        sp.dma_start(q_[r:r + HS * n, :, :], src.to_broadcast([n, HS, NH // 2 * T]))\
                          .then_inc(S["stacks_in"], 16)
                for e in range(2):
                    for first, n, part in RUNS:
                        for p in range(n if e == 0 and first == 0 else 0):
                            sp.wait_ge(part_out[1][p], 16 * (s + 2))
                        r = STACK * e + HS * first
                        sp.dma_start(k_[r:r + HS * n, e * NH // 2:(e + 1) * NH // 2, :],
                                     scratch[1, 0:n, e].rearrange("p d g t -> p d (g t)"))\
                          .then_inc(S["stacks_in"], 16)

            sp.dma_start(X[:, 0], x[0].rearrange("(t p) c -> p t c", p=128)).then_inc(x_in[0], 16)
            sp.dma_start(W64[:, :], w64).then_inc(S["w64_in"], 16)
            for b in range(1, 2):
                sp.dma_start(X[:, b], x[b].rearrange("(t p) c -> p t c", p=128)).then_inc(x_in[b], 16)
            sp.dma_start(boR[:, :], bo).then_inc(S["bo_in"], 16)
            store_parts(-2)
            load_stacks(-1)
            for b in range(2, B):
                sp.dma_start(X[:, b], x[b].rearrange("(t p) c -> p t c", p=128)).then_inc(x_in[b], 16)

            def job(s, par, on):
                for k in range(NG):
                    if k == 0 and on["v"] and s >= 0:
                        load_stacks(s)
                    if k == 3 and on["pre"]:
                        store_parts(s)

            slots(sp, job)
            for b in range(B):
                sp.wait_ge(S["odd_ready" if b % 2 else "even_ready"], b // 2 + 1)
                sp.dma_start(out[b].rearrange("(t p) c -> p t c", p=128), X[:, b]).then_inc(S["out_done"], 16)
            sp.wait_ge(S["out_done"], 16 * B)

        @block.gpsimd
        def _(pool):
            def low_part(j, name, s):
                wait(pool, name + "_mid", s + 3)
                pool.tensor_tensor(parts[:, j, 2], rest[:, j], parts[:, j, 1], ALU.subtract)\
                    .then_inc(S[name + "_lo"], 1)

            c = S["consts"]
            pool.memset(ident[:, :], 0.0).then_inc(c, 1)
            pool.memset(identb[:, :], 0.0).then_inc(c, 1)
            pool.memset(causal[:, :], 0.0).then_inc(c, 1)
            pool.memset(causalT[:, :], 0.0).then_inc(c, 1)
            pool.memset(expo[:, :], -0.5).then_inc(c, 1)
            pool.memset(onesR[:, :], 1.0).then_inc(c, 1)
            pool.wait_ge(c, 6)
            for m in (ident, identb):
                pool.affine_select(out=m[:, :], in_=m[:, :], compare_op=ALU.not_equal, fill=1.0, base=0,
                                   pattern=[[-1, 128]], channel_multiplier=1).then_inc(c, 1)
            pool.affine_select(out=causal[:, :], in_=causal[:, :], compare_op=ALU.is_ge, fill=MASKED, base=0,
                               pattern=[[-1, 128]], channel_multiplier=1).then_inc(c, 1)
            pool.affine_select(out=causalT[:, :], in_=causalT[:, :], compare_op=ALU.is_ge, fill=MASKED, base=0,
                               pattern=[[1, 128]], channel_multiplier=-1).then_inc(c, 1)
            pool.memset(Qs[0][:, :, :].bitcast(f32), 0.0).then_inc(S["q_zero"], 1)
            wait(pool, "var_done", 1)
            pool.tensor_tensor(rstd[:, 0], varp[:, 0], expo[:, :], ALU.pow).then_inc(S["rstd_done"], 1)
            pool.memset(Ks[1][:, :, :].bitcast(f32), 0.0).then_inc(S["ks1_zero"], 1)
            low_part(0, "q", -2)
            low_part(1, "k", -2)
            pool.memset(Qs[1][:, :, :].bitcast(f32), 0.0).then_inc(S["q_zero"], 1)
            for i in range(2):
                pool.memset(Va[i][:, :, :, :], 0.0).then_inc(S["va_zero"], 1)
            pool.wait_ge(S["va_zero"], 2)
            for i in range(2):
                pool.memset(Va[i][:, :, :, HS:HS + 1], 1.0).then_inc(S["va_zero"], 1)

            def power(j, var, done):
                pool.tensor_tensor(rstd[:, j], varp[:, j], expo[:, :], ALU.pow).then_inc(S[done], 1)

            def job(s, par, on):
                b = s - 1

                def gated():
                    wait(pool, "gate_done", 4)
                    for t in range(NT):
                        wait(pool, "y_scaled", NT * b + t + 1)
                        pool.tensor_tensor(y[:, t], y[:, t], gate[:, b, 0, :], ALU.mult).then_inc(S["ga_done"], 1)
                        if t:
                            add(t - 1)
                    add(NT - 1)

                def add(t):
                    wait(pool, "ga_done", NT * b + t + 1)
                    pool.tensor_tensor(X[:, b, t], X[:, b, t], y[:, t], ALU.add).then_inc(S["x1_done"], 1)

                for k in range(NG):
                    if k == 0 and on["pre"]:
                        wait(pool, "var_done", s + 3)
                        power(0, None, "rstd_done")
                    if k == 2 and on["post"]:
                        gated()
                    if k == 3 and on["pre"]:
                        low_part(0, "q", s)
                    if k == 2 and on["post"]:
                        wait(pool, "var2_done", s)
                        power(1, None, "rstd2_done")
                    if k == 3 and on["pre"]:
                        low_part(1, "k", s)

            slots(pool, job)
            for b in range(1, B, 2):
                pool.wait_ge(S["tanh_done"], b + 1)
                gb = gate[:, b, 1, :].unsqueeze(1).to_broadcast([128, NT, C])
                pool.tensor_tensor(zt[b], zt[b], gb, ALU.mult).then_inc(S["zgate_pool"], 1)
                pool.wait_ge(S["zgate_pool"], b // 2 + 1)
                pool.tensor_tensor(X[:, b], X[:, b], zt[b], ALU.add).then_inc(S["odd_ready"], 1)

        @block.scalar
        def _(act):
            act.dma_start(W[:, 0:at["wfT"][0]], w128[:, 0:at["wfT"][0]]).then_inc(S["w_a"], 16)
            act.dma_start(W[:, at["wmod"][0]:], w128[:, at["wmod"][0]:]).then_inc(S["w_mod"], 16)
            act.dma_start(W[:, at["wfT"][0]:at["wmod"][0]], w128[:, at["wfT"][0]:at["wmod"][0]])\
               .then_inc(S["w_rest"], 16)
            act.wait_ge(S["w_mod"], 16)
            act.activation(silu_t[:, :], w("cT"), ACT.Tanh, scale=0.5).then_inc(S["th_done"], 1)

            def turned(dst, made, copied, scale, shift, b, count, bank):
                wait(act, made, count)
                wait(act, "mod_done", 4)
                act.activation(dst[:, :], bank, ACT.Identity, bias=modc[:, shift, bass.ds(b, 1)],
                               scale=modc[:, scale, bass.ds(b, 1)]).then_inc(S[copied], 1)

            def high_part(j, name, s, bank=psM[:, :]):
                wait(act, name + "_made", s + 3)
                if s >= -1:
                    for p in range(PARTS):
                        act.wait_ge(part_out[j][p], 16 * (s + 2))
                act.activation(parts[:, j, 0], bank, ACT.Copy).then_inc(S[name + "_hi"], 1)

            def gate_act(dst, name, s, bias, scale):
                wait(act, name + "_made", s)
                wait(act, "s_done", s - 1)
                act.activation(dst[:, :], bank_of(s, name), ACT.Tanh, bias=bias, scale=scale)\
                   .then_inc(S[name + "_act"], 1)

            def y_copy(G, ypar, gk, b):
                wait(act, "pv_done", G + 1)
                wait(act, "y_turned", 4 * (b - 1))
                act.activation(Y[ypar][:, gk, :], psY[:, :], ACT.Copy).then_inc(S["y_copied"], 1)

            def job(s, par, on):
                for k in range(NG):
                    for i in range(B_ITEMS):
                        if on["b"]:
                            G = 4 * s + k
                            slot = (k + i) % 2
                            wait(act, "b_ready", B_ITEMS * G + i + 1)
                            if i == 0:
                                wait(act, "pv_done", G - 1)
                            act.activation(P[k % 2][:, 2 * i:2 * i + 2, :], psB[:, 2 * slot:2 * slot + 2, :],
                                           ACT.Exp, scale=SCALE).then_inc(S["exp_done"], 1)
                        if i == 0:
                            if k == 0 and on["post"]:
                                y_copy(4 * s - 2, 1 - par, 2, s - 1)
                            if k == 1 and on["post"]:
                                y_copy(4 * s - 1, 1 - par, 3, s - 1)
                            if k > 1 and on["b"]:
                                y_copy(4 * s + k - 2, par, k - 2, s)
                        if i == 2 and on["m"][k]:
                            G, gk = NG * s + k + 1, (k + 1) % NG
                            rows = psM[MAX_ROW:MAX_ROW + PARTS * HG, 0:T // 2].bitcast(bf16)
                            wait(act, "m_turned", G + 1)
                            act.activation(Qs[par if k < NG - 1 else 1 - par]
                                           [MAX_ROW:MAX_ROW + PARTS * HG, 2 * gk:2 * gk + 2, :],
                                           rows.unsqueeze(1).to_broadcast([PARTS * HG, 2, T]), ACT.Copy)\
                               .then_inc(S["m_copied"], 1)
                        if (k, i) == (0, 0) and on["post2"]:
                            wait(act, "z_made", s - 1)
                            act.activation(ZX[:, s - 2], bank_of(s, "z").rearrange("p (t c) -> p t c", t=NT), ACT.Copy)\
                               .then_inc(S["z_copied"], 1)
                        if (k, i) == (2, 1) and on["pre"]:
                            turned(hT, "h_turned", "h_copied", 1, 0, s + 2, s + 3, psM[:, :])
                        if (k, i) == (2, 3) and on["pre"]:
                            high_part(0, "q", s)
                        if (k, i) == (2, 4) and on["pre"]:
                            high_part(1, "k", s)
                        if (k, i) == (3, 0) and on["post"]:
                            turned(h2T, "h2_turned", "h2_copied", 3, 2, s - 1, s, bank_of(s, "h2"))
                        if (k, i) == (3, 1) and on["post"]:
                            gate_act(gf, "f", s, half_b[:, 0:1], 0.5)
                        if (k, i) == (3, 3) and on["post"]:
                            gate_act(gi, "i", s, half_b[:, 1:2], 0.5)
                        if (k, i) == (3, 4) and on["post"]:
                            gate_act(gg, "g", s, w("bc"), 1.0)

            turned(hT, "h_turned", "h_copied", 1, 0, 0, 1, psM[:, :])
            high_part(0, "q", -2, psB[:, 0, :])
            high_part(1, "k", -2, psB[:, 1, :])
            for n, bank in enumerate((2, 3, 0, 1)):
                act.wait_ge(S["gate_made"], n + 1)
                act.activation(gate[:, 2 * bank:2 * bank + 2],
                               psB[:, bank, :].rearrange("p (b j c) -> p b j c", b=2, j=2), ACT.Copy)\
                   .then_inc(S["gate_done"], 1)
            for i in range(2):
                act.wait_ge(S[f"ks{i}_zero"], 1)
                act.dma_start(Ks[i][MAX_ROW:MAX_ROW + PARTS * HG, :, :], sel.bitcast(bf16)).then_inc(S["sel_in"], 16)
            slots(act, job)
            for b in range(B):
                act.wait_ge(S["zsum_done"], b + 1)
                act.activation(zt[b], ZX[:, b], ACT.Tanh).then_inc(S["tanh_done"], 1)

        @block.vector
        def _(dve):
            sv = [0]

            def done_setup(ins):
                sv[0] += 1
                ins.then_inc(S["setup_v"], 1)
                return sv[0]

            def norm_stats(j, b, two, count):
                if not two and isinstance(b, int):
                    dve.wait_ge(x_in[b], 16)
                for t in range(NT):
                    if two:
                        wait(dve, "x1_done", NT * b + t + 1)
                    last = dve.bn_stats(stat[:, j, t, :], X[:, b, t, :])
                last.then_inc(S[f"stat{two}_done"], 1)
                wait(dve, f"stat{two}_done", count)
                for t in range(NT):
                    last = dve.bn_aggr(mv[:, j, t, :], stat[:, j, t, :])
                last.then_inc(S[f"stat{two}_done"], 1)
                return

            def norm_var(j, two, count):
                wait(dve, f"stat{two}_done", 2 * count)
                dve.tensor_scalar(varp[:, j], mv[:, j, :, 1], EPS, None, ALU.add).then_inc(S[f"var{two}_done"], 1)

            def norm_apply(j, b, two, count):
                wait(dve, f"rstd{two}_done", count)
                for t in range(NT):
                    last = dve.tensor_scalar(xn[:, j, t], X[:, b, t, :], mv[:, j, t, 0:1], rstd[:, j, t:t + 1],
                                             ALU.subtract, ALU.mult)
                last.then_inc(S[f"xn{two}_done"], 1)

            def rest_parts(j, name, s, bank=psM[:, :]):
                wait(dve, name + "_hi", s + 3)
                dve.tensor_tensor(rest[:, j], bank, parts[:, j, 0], ALU.subtract)\
                   .then_inc(S[name + "_rest"], 1)
                wait(dve, name + "_rest", s + 3)
                dve.tensor_copy(parts[:, j, 1], rest[:, j]).then_inc(S[name + "_mid"], 1)

            def reduce_item(G, kk, i):
                wait(dve, "a_ready", A_ITEMS * G + i + 1)
                bank = psA[:, i % 2, :].rearrange("p (n c) -> p n c", n=4)
                d = bm[:, kk % 2]
                if i < 4:
                    o = d[:, i, 3, :]
                elif i < 8:
                    o = d[:, i - 4].rearrange("p a b -> p (a b)")[:, 1:5]
                else:
                    o = d[:, 2 * (i - 8):2 * (i - 8) + 2, 2, 0:2]
                dve.tensor_reduce(o, bank, AX.X, ALU.max).then_inc(S["a_reduced"], 1)

            def finish_max(G, kk):
                wait(dve, "a_reduced", A_ITEMS * (G + 1))
                dve.tensor_reduce(nm[:, kk % 2], bm[:, kk % 2], AX.X, ALU.max, negate=True)\
                   .then_inc(S["nm_done"], 1)

            def part1(G, kk):
                wait(dve, "nm_done", G + 1)
                wait(dve, "m_turned", G - 1)
                dve.tensor_copy(nparts[:, kk % 2, :, 0, :], nm[:, kk % 2].rearrange("p h t -> p t h"))\
                   .then_inc(S["n_part"], 1)

            def part1r(G, kk):
                wait(dve, "n_part", 2 * G + 1)
                dve.tensor_tensor(nr[:, kk % 2], nm[:, kk % 2],
                                  nparts[:, kk % 2, :, 0, :].rearrange("p t h -> p h t"), ALU.subtract)\
                   .then_inc(S["nr_done"], 1)

            def part2(G, kk):
                wait(dve, "nr_done", G + 1)
                dve.tensor_copy(nparts[:, kk % 2, :, 1, :], nr[:, kk % 2].rearrange("p h t -> p t h"))\
                   .then_inc(S["n_part"], 1)

            def part3(G, kk):
                wait(dve, "n_part", 2 * G + 2)
                dve.tensor_tensor(nparts[:, kk % 2, :, 2, :], nr[:, kk % 2].rearrange("p h t -> p t h"),
                                  nparts[:, kk % 2, :, 1, :], ALU.subtract).then_inc(S["n_ready"], 1)

            small = [finish_max, part1, part1r, part2, part3]

            def scale_y(t, b, bank):
                wait(dve, "y_turned", 4 * b + t + 1)
                t_ = bank.rearrange("p (h d) -> p h d", d=32)
                dve.reciprocal(rden[:, t], t_[:, :, HS]).then_inc(S["r_done"], 1)
                wait(dve, "r_done", 4 * b + t + 1)
                if t == 0:
                    wait(dve, "x1_done", NT * b)
                dve.tensor_tensor(y[:, t].rearrange("p (h d) -> p h d", d=HS), t_[:, :, 0:HS],
                                  rden[:, t].unsqueeze(2).to_broadcast([128, NH, HS]), ALU.mult)\
                   .then_inc(S["y_scaled"], 1)

            def job(s, par, on):
                for k in range(NG):
                    for i in range(A_ITEMS):
                        if on["a"][k]:
                            reduce_item(4 * s + k + LEAD, k, i)
                        G1 = 4 * s + k + LEAD - 1
                        prev = on["m"][k]
                        if i < 5 and prev:
                            small[i](G1, k + 1)
                        if (k, i) == (0, 1) and on["post2"]:
                            wait(dve, "g_act", s - 1)
                            wait(dve, "i_act", s - 1)
                            dve.scalar_tensor_tensor(out=gi[:, :], in0=gi[:, :], scalar=1.0, in1=gg[:, :],
                                                     op0=ALU.add, op1=ALU.mult).then_inc(S["v_done"], 1)
                        if (k, i) == (0, 2) and on["post2"]:
                            wait(dve, "v_done", s - 1)
                            wait(dve, "u_done", s - 1)
                            dve.scalar_tensor_tensor(out=sT[:, :], in0=gf[:, :], scalar=0.5, in1=gi[:, :],
                                                     op0=ALU.mult, op1=ALU.add).then_inc(S["s_done"], 1)
                        if (k, i) == (0, 3) and on["pre"]:
                            norm_stats(0, s + 2, "", 2 * (s + 2) + 1)
                        if (k, i) == (0, 4) and on["pre"]:
                            norm_var(0, "", s + 3)
                        if (k, i) == (0, 9) and on["pre"]:
                            norm_apply(0, s + 2, "", s + 3)
                        if (k, i) == (1, 1) and on["v"]:
                            wait(dve, "v_made", s + 2)
                            wait(dve, "pv_done", 4 * s)
                            if isinstance(s, int) and s < 1:
                                dve.wait_ge(S["va_zero"], 4)
                            dve.tensor_copy(Va[1 - par][:, :, :, 0:HS],
                                            psM[:, :].rearrange("p (t h d) -> p t h d", t=NT, d=HS))\
                               .then_inc(S["v_copied"], 1)
                        if on["post"] and (k, i) in ((1, 3), (1, 7), (1, 9), (2, 1)):
                            t = ((1, 3), (1, 7), (1, 9), (2, 1)).index((k, i))
                            scale_y(t, s - 1, bank_of(s, "y", t))
                        if (k, i) == (2, 5) and on["post"]:
                            norm_stats(1, s - 1, "2", 2 * (s - 1) + 1)
                        if (k, i) == (2, 6) and on["post"]:
                            norm_var(1, "2", s)
                        if (k, i) == (2, 8) and on["pre"]:
                            rest_parts(0, "q", s)
                        if (k, i) == (2, 9):
                            if on["post"]:
                                norm_apply(1, s - 1, "2", s)
                            if on["pre"]:
                                rest_parts(1, "k", s)
                        if (k, i) == (3, 5) and on["post"]:
                            wait(dve, "f_act", s)
                            dve.scalar_tensor_tensor(out=gf[:, :], in0=gf[:, :], scalar=1.0, in1=sT[:, :],
                                                     op0=ALU.add, op1=ALU.mult).then_inc(S["u_done"], 1)

            for j in range(2):
                done_setup(dve.memset(bm[:, j], LOWEST))
            zeroed = done_setup(dve.memset(sT[:, :], 0.0))
            dve.memset(Ks[0][:, :, :].bitcast(f32), 0.0).then_inc(S["ks0_zero"], 1)
            norm_stats(0, 0, "", 1)
            norm_var(0, "", 1)
            dve.wait_ge(S["th_done"], 1)
            dve.scalar_tensor_tensor(out=silu[:, :], in0=silu_t[:, :], scalar=1.0, in1=w("cT"),
                                     op0=ALU.add, op1=ALU.mult).then_inc(S["silu_done"], 1)
            dve.wait_ge(S["setup_mm"], 1)
            done_setup(dve.tensor_copy(WQ[:, :], psA[:, 0, 0:C]))
            done_setup(dve.tensor_copy(AT[:, :], psA[:, 1, 0:C]))
            assert done_setup(dve.tensor_copy(VE[:, :], psY[0:KVL, 0:C])) == 6
            norm_apply(0, 0, "", 1)
            dve.wait_ge(S["mod_made"], 1)
            mod = psM[:, 0:6 * B].rearrange("p (j b) -> p j b", j=6)
            for half in range(2):
                dve.tensor_scalar(modc[:, 2 * half], mod[:, 3 * half], 0.5, None, ALU.mult)\
                   .then_inc(S["mod_done"], 1)
                dve.tensor_scalar(modc[:, 2 * half + 1], mod[:, 3 * half + 1], 0.5, 1.0, ALU.mult, ALU.add)\
                   .then_inc(S["mod_done"], 1)
            raw = done_setup(dve.tensor_scalar(gcol[:, :, :], mod[:, 2:6:3], 0.5, None, ALU.mult))
            assert raw == 7
            dve.wait_ge(S["setup_mm"], 2)
            done_setup(dve.tensor_copy(KE[:, :], psB[0:KVL, 2, 0:C]))
            assert done_setup(dve.tensor_copy(WV[:, :], psB[:, 3, 0:C])) == 9
            dve.wait_ge(S["setup_v"], raw)
            done_setup(dve.tensor_scalar(gsign[:, :, :], gcol[:, :, :], 0.0, 2.0, ALU.is_ge, ALU.mult))
            n = done_setup(dve.scalar_tensor_tensor(out=gabs[:, :, :], in0=gcol[:, :, :], scalar=-1.0,
                                                    in1=gcol[:, :, :], op0=ALU.mult, op1=ALU.max))
            dve.wait_ge(S["setup_v"], n)
            n = done_setup(dve.tensor_scalar(gabs[:, :, :], gabs[:, :, :], 0.25, None, ALU.max))
            dve.wait_ge(S["setup_mm"], 3)
            done_setup(dve.tensor_copy(WK[:, :], psB[:, 1, 0:C]))
            dve.wait_ge(S["setup_v"], n)
            dve.scalar_tensor_tensor(out=gcol[:, :, :], in0=gsign[:, :, :], scalar=-1.0, in1=gabs[:, :, :],
                                     op0=ALU.add, op1=ALU.mult).then_inc(S["gcol_done"], 1)
            rest_parts(0, "q", -2, psB[:, 0, :])
            rest_parts(1, "k", -2, psB[:, 1, :])
            dve.wait_ge(S["w_rest"], 16)
            dve.wait_ge(S["setup_v"], zeroed)
            dve.tensor_scalar(sT[:, :], sT[:, :], w("in_c"), 2.0, ALU.add, ALU.mult).then_inc(S["state_set"], 1)
            dve.tensor_scalar(half_b[:, :], W[:, at["bf"][0]:at["bi"][1]], 0.5, None, ALU.mult)\
               .then_inc(S["state_set"], 1)
            u4 = W[:, at["ufT"][0]:at["uoT"][1]]
            dve.tensor_scalar(u4, u4, 0.5, None, ALU.mult).then_inc(S["state_set"], 1)

            slots(dve, job)
            dve.wait_ge(S["z_copied"], B)
            dve.wait_ge(S["cu_made"], 1)
            cu = psB[:, 1, :].rearrange("p (t c) -> p t c", t=NT)

            def finish_even(b):
                dve.wait_ge(S["tanh_done"], b + 1)
                gb = gate[:, b, 1, :].unsqueeze(1).to_broadcast([128, NT, C])
                dve.tensor_tensor(zt[b], zt[b], gb, ALU.mult).then_inc(S["zgate_done"], 1)
                dve.wait_ge(S["zgate_done"], b // 2 + 1)
                dve.tensor_tensor(X[:, b], X[:, b], zt[b], ALU.add).then_inc(S["even_ready"], 1)

            for b in range(B):
                dve.tensor_tensor(ZX[:, b], ZX[:, b], cu, ALU.add).then_inc(S["zsum_done"], 1)
                if b >= 3 and b % 2:
                    finish_even(b - 3)
            finish_even(B - 2)

        @block.tensor
        def _(pe):
            def mm(o, l, r, start=True, stop=True):
                return pe.matmul(o, l, r, start=start, stop=stop)

            pe.wait_ge(S["w64_in"], 16)
            pe.wait_ge(S["w_a"], 16)
            mm(psA[:, 0, 0:C], W_dq, W_uqT)
            mm(psA[:, 1, 0:C], W_uqT, W_dq)
            mm(psY[0:KVL, 0:C], w("W_uv"), w("W_oT")).then_inc(S["setup_mm"], 1)
            pe.wait_ge(S["silu_done"], 1)
            wm = w("wmod").rearrange("p (j c) -> p j c", j=6)
            for j in range(6):
                last = mm(psM[:, j * B:(j + 1) * B], wm[:, j], silu[:, :])
            last.then_inc(S["mod_made"], 1)
            pe.wait_ge(S["setup_v"], 6)
            mm(psB[0:KVL, 2, 0:C], w("W_uk"), AT[:, :])
            mm(psB[:, 3, 0:C], W_dkv, VE[:, :]).then_inc(S["setup_mm"], 1)
            pe.wait_ge(S["consts"], 10)
            pe.wait_ge(S["mod_done"], 4)
            pe.wait_ge(S["setup_v"], 7)
            pe.wait_ge(S["xn_done"], 1)
            for t in range(NT):
                last = pe.transpose(psM[:, t * 128:(t + 1) * 128], xn[:, 0, t], ident[:, :])
            last.then_inc(S["h_turned"], 1)
            pe.wait_ge(S["setup_v"], 9)
            mm(psB[:, 1, 0:C], W_dkv, KE[:, :]).then_inc(S["setup_mm"], 1)
            pe.wait_ge(S["h_copied"], 1)
            mm(psB[:, 0, :], WQ[:, :], hT[:, :]).then_inc(S["q_made"], 1)
            pe.wait_ge(S["setup_v"], 13)
            mm(psB[:, 1, :], WK[:, :], hT[:, :]).then_inc(S["k_made"], 1)
            pe.wait_ge(S["gcol_done"], 1)
            for bank in (2, 3, 0, 1):
                if bank == 0:
                    pe.wait_ge(S["k_rest"], 1)
                for n in range(4):
                    b, j = 2 * bank + n // 2, n % 2
                    last = mm(psB[:, bank, n * 128:(n + 1) * 128],
                              gcol[:, j, b:b + 1].to_broadcast([128, 128]), ident[:, :])
                last.then_inc(S["gate_made"], 1)
            pe.wait_ge(S["gate_done"], 4)

            def scores_max(G, gk, bpar, i):
                wait(pe, "a_reduced", A_ITEMS * G + i - 1)
                q_, k_ = Qs[bpar], Ks[bpar]
                bank = psA[:, i % 2, :]

                def tile(h, t, c0):
                    n_ = (t + 1) * 128
                    hh = gk * HG + h
                    mm(bank[:, c0:c0 + n_], q_[0:MAX_ROW, hh // 2, t * 128:(t + 1) * 128], k_[0:MAX_ROW, key_at(hh), 0:n_],
                       True, False)
                    return mm(bank[:, c0 + n_ - 128:c0 + n_], identb[:, :], causal[:, :], False, True)

                if i < 4:
                    last = tile(i, 3, 0)
                elif i < 8:
                    tile(i - 4, 2, 0)
                    last = tile(i - 4, 0, 384)
                else:
                    tile(2 * (i - 8), 1, 0)
                    last = tile(2 * (i - 8) + 1, 1, 256)
                last.then_inc(S["a_ready"], 1)

            def scores(G, k, bpar, i):
                wait(pe, "exp_done", B_ITEMS * G + i - 1)
                q_, k_ = Qs[bpar], Ks[bpar]
                slot = (k + i) % 2

                def tile(h, kb, bank, c0):
                    hh = k * HG + h
                    mm(psB[:, 2 * slot + bank, c0:c0 + T - kb * 128],
                       k_[:, key_at(hh), kb * 128:(kb + 1) * 128], q_[:, hh // 2, kb * 128:T], True, False)
                    return mm(psB[:, 2 * slot + bank, c0:c0 + 128], identb[:, :], causalT[:, :], False, True)

                for bank in range(2):
                    if i < 2:
                        last = tile(2 * i + bank, 0, bank, 0)
                    elif i < 4:
                        h = 2 * (i - 2) + bank
                        tile(h, 1, bank, 0)
                        last = tile(h, 3, bank, 384)
                    else:
                        tile(2 * bank, 2, bank, 0)
                        last = tile(2 * bank + 1, 2, bank, 256)
                last.then_inc(S["b_ready"], 1)

            def p_view(p_, h, kb):
                if kb == 0:
                    return p_[:, h, 0:512]
                if kb == 1:
                    return p_[:, 4 + h, 0:384]
                if kb == 3:
                    return p_[:, 4 + h, 384:512]
                return p_[:, 8 + h // 2, (h % 2) * 256:(h % 2) * 256 + 256]

            def values(G, gk, bpar, kb):
                if kb == 0:
                    wait(pe, "exp_done", B_ITEMS * (G + 1))
                    wait(pe, "y_copied", G)
                for h in range(HG):
                    last = mm(psY[32 * h:32 * h + 32, kb * 128:T], Va[bpar][:, kb, gk * HG + h, :],
                              p_view(P[gk % 2], h, kb), kb == 0, kb == NT - 1)
                if kb == NT - 1:
                    last.then_inc(S["pv_done"], 1)

            def job(s, par, on):
                def max_rows(k):
                    G = 4 * s + k + 1
                    misc_free(pe, s, on, ("m", k))
                    wait(pe, "n_ready", G + 1)
                    for seg, t in enumerate((2, 0, 1, 3)):
                        o = psM[MAX_ROW:MAX_ROW + PARTS * HG, t * 64:(t + 1) * 64].bitcast(bf16)
                        last = pe.transpose(o, nparts[:, (k + 1) % 2, seg].rearrange("p a h -> p (a h)"),
                                            identb[:, :])
                    last.then_inc(S["m_turned"], 1)

                def turn(dst_j, name, ready, count, jb):
                    bank = bank_of(s, *jb)
                    misc_free(pe, s, on, jb)
                    wait(pe, ready, count)
                    for t in range(NT):
                        last = pe.transpose(bank[:, t * 128:(t + 1) * 128], xn[:, dst_j, t], ident[:, :])
                    last.then_inc(S[name], 1)

                def project(weight, name, jb, count):
                    misc_free(pe, s, on, jb)
                    wait(pe, "h_copied", count)
                    mm(psM[:, :], weight, hT[:, :]).then_inc(S[name], 1)

                def turn_y(t):
                    misc_free(pe, s, on, ("y", t))
                    wait(pe, "y_copied", 4 * s)
                    for g in range(NG):
                        last = pe.transpose(bank_of(s, "y", t)[:, g * 128:(g + 1) * 128],
                                            Y[1 - par][:, g, t * 128:(t + 1) * 128], ident[:, :])
                    last.then_inc(S["y_turned"], 1)

                def gate_state(name, bank, first):
                    wait(pe, "state_set", 3)
                    wait(pe, "s_done", s - 1)
                    return mm(bank, w("u" + name), sT[:, :], first, not first)

                def gate_input(name, bank, first):
                    wait(pe, "h2_copied", s)
                    return mm(bank, w("w" + name), h2T[:, :], first, not first)

                def gate_mm(weights, name):
                    misc_free(pe, s, on, (name, 0))
                    bank = bank_of(s, name)
                    gate_input(weights, bank, True)
                    gate_state(weights, bank, False).then_inc(S[name + "_made"], 1)

                for k in range(NG):
                    for i in range(B_ITEMS):
                        if on["b"]:
                            if k == 0 and i == 0 and isinstance(s, int) and s == 0:
                                pe.wait_ge(S["sel_in"], 32)
                            if i == 0:
                                wait(pe, "m_copied", NG * s + k + 1)
                            scores(4 * s + k, k, par, i)
                        if on["a"][k]:
                            G = 4 * s + k + LEAD
                            if k == 2 and i == 0:
                                wait(pe, "stacks_in", LOADS * (s + 2))
                            for a in range(2):
                                scores_max(G, (k + LEAD) % 4, par if k < 2 else 1 - par, 2 * i + a)
                        if i > 0:
                            if k == 0 and on["post"]:
                                values(4 * s - 1, 3, 1 - par, i - 1)
                            if k > 0 and on["b"]:
                                values(4 * s + k - 1, k - 1, par, i - 1)
                        if (k, i) == (0, 0) and on["post2"]:
                            misc_free(pe, s, on, ("z", 0))
                            for t in range(NT):
                                last = mm(bank_of(s, "z")[:, t * 128:(t + 1) * 128], h2T[:, t * 128:(t + 1) * 128],
                                          w("woT"))
                            last.then_inc(S["z_made"], 1)
                        if (k, i) == (1, 0) and on["v"]:
                            misc_free(pe, s, on, ("v", 0))
                            wait(pe, "h_copied", s + 2)
                            for t in range(NT):
                                last = mm(psM[:, t * 128:(t + 1) * 128], hT[:, t * 128:(t + 1) * 128], WV[:, :])
                            last.then_inc(S["v_made"], 1)
                        if i == 2 and on["m"][k]:
                            max_rows(k)
                        if on["post"] and (k, i) in ((1, 1), (1, 3), (1, 4), (2, 0)):
                            turn_y(((1, 1), (1, 3), (1, 4), (2, 0)).index((k, i)))
                        if (k, i) == (2, 1) and on["pre"]:
                            turn(0, "h_turned", "xn_done", s + 3, ("h", 0))
                        if (k, i) == (2, 3) and on["pre"]:
                            project(WQ[:, :], "q_made", ("q", 0), s + 3)
                        if (k, i) == (2, 4) and on["pre"]:
                            project(WK[:, :], "k_made", ("k", 0), s + 3)
                        if (k, i) == (3, 0) and on["post"]:
                            turn(1, "h2_turned", "xn2_done", s, ("h2", 0))
                        if (k, i) == (3, 1) and on["post"]:
                            gate_mm("fT", "f")
                        if (k, i) == (3, 3) and on["post"]:
                            gate_mm("iT", "i")
                        if (k, i) == (3, 4) and on["post"]:
                            gate_mm("cT", "g")

            slots(pe, job)
            pe.wait_ge(S["s_done"], B)
            pe.wait_ge(S["bo_in"], 16)
            pe.wait_ge(S["y_scaled"], NT * B)
            for t in range(NT):
                o = psB[:, 1, t * 128:(t + 1) * 128]
                mm(o, sT[:, t * 128:(t + 1) * 128], w("uoT"), True, False)
                last = mm(o, onesR[:, :], boR[:, :], False, True)
            last.then_inc(S["cu_made"], 1)


def kernel(**inputs):
    import concourse.bacc as bacc
    from concourse.bass_utils import run_bass_kernel_spmd

    a = {k.replace("L0_", "").replace("attn_", "").replace("ffn_", ""): np.asarray(v) for k, v in inputs.items()}
    col = {"W_uk": a["W_uk"], "W_uv": a["W_uv"], "W_oT": a["W_o"].T, "wmod": a["wmod"], "cT": a["c"].T}
    for n in ("wf", "wi", "wc", "wo", "uf", "ui", "uc", "uo"):
        col[n + "T"] = a[n].T
    for n in ("bf", "bi", "bc", "in_c"):
        col[n] = a[n][:, None]
    arrays = {
        "x": np.ascontiguousarray(a["x"]),
        "w64": np.ascontiguousarray(np.concatenate([a["W_dq"], a["W_uq"].T, a["W_dkv"]], axis=1)),
        "w128": np.ascontiguousarray(np.concatenate([col[n] for n in W128], axis=1)),
        "bo": np.ascontiguousarray(a["bo"][None, :]),
    }
    heads = np.concatenate([np.arange(0, NH, 2), np.arange(1, NH, 2)])
    own = (np.arange(PARTS * HG)[:, None] % HG) == (heads[None, :] % HG)
    arrays["sel"] = np.repeat(own[:, :, None], T, axis=2).astype(np.uint16) * ONE_BF16
    nc = bacc.Bacc("TRN2", target_bir_lowering=False, num_devices=1)
    f32 = mybir.dt.float32
    aps = [nc.dram_tensor(k, v.shape, mybir.dt.from_np(v.dtype), kind="ExternalInput").ap()
           for k, v in arrays.items()]
    scratch = nc.dram_tensor("scratch", [2, PARTS, 2, HS, NH // 2, T], mybir.dt.bfloat16, kind="Internal").ap()
    out = nc.dram_tensor("out", [B, T, C], f32, kind="ExternalOutput").ap()
    build(nc, *aps, scratch, out)
    r = run_bass_kernel_spmd(nc, [arrays], core_ids=[0])
    return r.results[0]["out"]
```

```python
from contextlib import ExitStack

import numpy as np

import concourse.bass as bass
from concourse import mybir

B, T, C = 8, 512, 128
NH, HS, KVL = 16, 8, 64
NT = T // 128
HG = 4
NG = NH // HG
PARTS = 3
PAIRS = ((0, 0), (0, 1), (0, 2), (1, 0), (1, 1), (2, 0))
STACK = len(PAIRS) * HS
MAX_ROW = 2 * STACK
A_ITEMS = 10
RUNS = ((0, 3, 0), (3, 2, 1), (5, 1, 2))
LOADS = 16 * 12
B_ITEMS = 5
HV = HS + 1
SET = 32 // HV
SETS = -(-NG // SET)
V_AT = HV * (SET - 1)
YT = 2
NY = NT // YT
LEAD = 2
M_AT = (2, 2, 2, 2)
Q_STEP = ((2, 1), (2, 2))
K_STEP = ((2, 3), (2, 4))
LATE_SECOND = ((0, 3), (0, 4))
SCALE = float(HS) ** -0.5
EPS = 1e-5
MASKED = -1.0e30
LOWEST = -3.0e38
ONE_BF16 = np.uint16(0x3F80)

W128 = ["W_uk", "W_uv", "W_oT", "wfT", "wiT", "wcT", "ufT", "uiT", "ucT", "wmod", "cT", "woT", "uoT",
        "bf", "bi", "bc", "in_c"]
WIDTH = dict(W_uk=KVL, W_uv=KVL, wmod=6 * C, cT=B, bf=1, bi=1, bc=1, in_c=1)


def build(nc, x, w64, w128, bo, sel, scratch, out):
    f32, bf16, f32r = mybir.dt.float32, mybir.dt.bfloat16, mybir.dt.float32r
    ALU, ACT, AX = mybir.AluOpType, mybir.ActivationFunctionType, mybir.AxisListType

    at, n = {}, 0
    for name in W128:
        at[name] = (n, n + WIDTH.get(name, C))
        n = at[name][1]
    w128_cols = n
    set_up = at["cT"][1]

    with ExitStack() as ctx:
        def sb(name, shape, dt=f32):
            return ctx.enter_context(nc.sbuf_tensor(name, shape, dt))

        def ps(name, shape):
            return ctx.enter_context(nc.psum_tensor(name, shape, f32))

        def sem(name):
            return ctx.enter_context(nc.semaphore(name))

        W64 = sb("W64", [KVL, 3 * C])
        W_kept = sb("W_kept", [128, w128_cols - set_up])
        boR = sb("boR", [1, C])
        onesR = sb("onesR", [1, 128])
        ident = sb("ident", [128, 128])
        identb = sb("identb", [128, 128], bf16)
        causal = sb("causal", [128, 128], bf16)
        causalT = sb("causalT", [128, 128], bf16)
        AT = sb("AT", [128, C])
        VE = sb("VE", [KVL, C])
        KE = sb("KE", [KVL, C])
        WQ = sb("WQ", [128, C])
        WK = sb("WK", [128, C])
        WV = sb("WV", [128, C])
        silu_t = sb("silu_t", [128, B])
        silu = sb("silu", [128, B])
        modc = sb("modc", [128, 4, B])
        gcol = sb("gcol", [128, 2, B])
        gsign = sb("gsign", [128, 2, B])
        gabs = sb("gabs", [128, 2, B])
        gate = sb("gate", [128, B, 2, C])
        half_b = sb("half_b", [128, 2])
        expo = sb("expo", [128, NT])
        X = sb("X", [128, B, NT, C])
        ZX = sb("ZX", [128, B, NT, C])
        stat = sb("stat", [128, 2, NT, 6])
        mv = sb("mv", [128, 2, NT, 2])
        varp = sb("varp", [128, 2, NT])
        rstd = sb("rstd", [128, 2, NT])
        xn = sb("xn", [128, 2, NT, C])
        hT = sb("hT", [128, T])
        h2T = sb("h2T", [128, T])
        halves = {name: [sb(f"{name}_{part}", [128, T], f32r) for part in ("high", "low")] for name in ("h", "s")}
        halves["h2"] = halves["h"]
        QK_high = sb("QK_high", [128, 2, C], f32r)
        QK_low = sb("QK_low", [128, 2, C], f32r)
        W_high = sb("W_high", [128, 6 * C], f32r)
        W_low = sb("W_low", [128, 6 * C], f32r)
        parts = sb("parts", [128, 2, PARTS, T], bf16)
        rest = sb("rest", [128, 2, T])
        Qs = [sb(f"Qs{i}", [128, NH // 2, T], bf16) for i in range(2)]
        Ks = [sb(f"Ks{i}", [128, NH, T], bf16) for i in range(2)]
        Va = [sb(f"Va{i}", [128, NT, NH + 1, 32]) for i in range(2)]
        bm = sb("bm", [128, 2, HG, NT, 4])
        nm = sb("nm", [128, 2, HG, NT])
        nr = sb("nr", [128, 2, HG, NT])
        nparts = sb("nparts", [128, 2, NT, PARTS, HG], bf16)
        P = [sb(f"P{i}", [128, 10, T]) for i in range(2)]
        W_set_up = P[1][:, :, :].rearrange("p a t -> p (a t)")[:, 0:set_up]
        zt = [P[0][:, i, :].rearrange("p (t c) -> p t c", t=NT) for i in range(B)]
        Y = [sb(f"Y{i}", [128, SETS, T]) for i in range(2)]
        rden = sb("rden", [128, NT, HG, NG])
        y = sb("y", [128, NT, C])
        gf = sb("gf", [128, T])
        gi = sb("gi", [128, T])
        gg = sb("gg", [128, T])
        sT = sb("sT", [128, T])

        psA = ps("psA", [128, 2, 512])
        psB = ps("psB", [128, 4, 512])
        psY = ps("psY", [128, 512])
        psM = ps("psM", [128, 512])

        names = """gate_made centred centred2 w64_in bo_in consts setup_mm setup_v th_done silu_done mod_made state_set mod_done gate_done
            w_high w_split qk_high qk_split h_high h_low h2_high h2_low s_high s_low
            stat_done rstd_done xn_done var_done h_turned h_copied q_made q_hi q_copied k_copied q_rest q_mid q_lo k_made k_hi k_rest
            k_mid k_lo v_made v_copied stacks_in a_ready a_reduced nm_done n_part nr_done n_ready
            m_turned m_copied q_zero ks0_zero ks1_zero va_zero gcol_done sel_in w_a w_mod w_rest b_ready exp_done  pv_done y_copied y_turned yt_copied r_done y_scaled
            ga_done x1_done h2_turned h2_copied f_made i_made g_made f_act i_act g_act u_done v_done s_done
            z_made z_copied cu_made zsum_done tanh_done zgate_pool zgate_done pool_ready dve_ready out_done""".split()
        S = {k: sem(k) for k in names}
        x_in = [sem(f"x_in{b}") for b in range(B)]
        part_out = [[sem(f"{name}{p}_out") for p in range(PARTS)] for name in "qk"]
        S["stat2_done"], S["rstd2_done"], S["xn2_done"], S["var2_done"] = (
            sem("stat2_done"), sem("rstd2_done"), sem("xn2_done"), sem("var2_done"))

        block = ctx.enter_context(nc.Block())
        LAST_ORDER = [b + 1 - 2 * (b % 2) for b in range(B)]
        POOL_SHARE = [(b, slice(0, NT)) for b in range(1, B - 1, 2)] + [(B - 1, slice(NT // 2, NT))]
        DVE_SHARE = [(b, slice(0, NT)) for b in range(0, B, 2)] + [(B - 1, slice(0, NT // 2))]
        mod = psM[:, 0:6 * B].rearrange("p (j b) -> p j b", j=6)
        AT_VE, AT_VE_WQ, AT_VE_WQ_KE, ALL_WEIGHTS = 5, 6, 7, 9

        def wait(e, name, value):
            if isinstance(value, int) and value <= 0:
                return
            e.wait_ge(S[name], value)

        def key_at(h):
            return (h % 2) * (NH // 2) + h // 2

        def w(name):
            return columns(name, name)

        def columns(first, last):
            c0, c1 = at[first][0], at[last][1]
            return W_set_up[:, c0:c1] if c1 <= set_up else W_kept[:, c0 - set_up:c1 - set_up]

        def gate_halves(name):
            c0, c1 = (c - at["wfT"][0] for c in at[name])
            return W_high[:, c0:c1], W_low[:, c0:c1]

        turned_out = (gi, gg)

        W_dq, W_uqT, W_dkv = (W64[:, i * C:(i + 1) * C] for i in range(3))

        def on_of(s):
            return dict(pre=0 <= s + 2 < B, v=0 <= s + 1 < B, b=0 <= s < B, post=0 <= s - 1 < B,
                        post2=0 <= s - 2 < B,
                        a=[0 <= NG * s + k + LEAD < NG * B for k in range(NG)],
                        m=[0 <= NG * s + k + 1 < NG * B for k in range(NG)])

        def slots(e, job):
            for s in range(-1, B + 2):
                job(s, s % 2, on_of(s))

        def misc_users(s, on):
            order = []
            if isinstance(s, int) and s == -2:
                return [(("h", 0), "h_copied", 1)]

            def use(stage, kind, i, copied, count):
                if stage:
                    order.append(((kind, i), copied, count))

            use(on["m"][0], "m", 0, "m_copied", 4 * s + 2)
            use(on["post2"], "z", 0, "z_copied", s - 1)
            use(on["v"], "v", 0, "v_copied", s + 2)
            use(on["post"], "y", 0, "yt_copied", NY * (s - 1) + 1)
            use(on["post"], "y", 1, "yt_copied", NY * (s - 1) + 2)
            use(on["m"][1], "m", 1, "m_copied", 4 * s + 3)
            use(on["pre"], "h", 0, "h_high", s + 2)
            use(on["pre"], "q", 0, "q_copied", s + 2)
            use(on["m"][2], "m", 2, "m_copied", 4 * s + 4)
            use(on["pre"], "k", 0, "k_copied", s + 2)
            use(on["post"], "h2", 0, "h2_high", s)
            use(on["post"], "f", 0, "f_act", s)
            use(on["m"][3], "m", 3, "m_copied", 4 * s + 5)
            use(on["post"], "i", 0, "i_act", s)
            use(on["post"], "g", 0, "g_act", s)
            return order

        LAST_BANKS = {
            B: {("y", t): (psB[:, t, :], ("exp_done", B_ITEMS * NG * B)) for t in range(NY)},
            B + 1: {("z", 0): (psB[:, 0, :], ("y_scaled", NY * B))},
        }
        LAST_BANKS[B][("f", 0)] = (psA[:, 0, :], ("a_reduced", A_ITEMS * NG * B))
        LAST_BANKS[B][("i", 0)] = (psA[:, 1, :], ("a_reduced", A_ITEMS * NG * B))
        LAST_BANKS[B][("g", 0)] = (psY[:, :], ("y_copied", SETS * B))
        LAST_BANKS[B][("h2", 0)] = (psM[:, :], ("z_copied", B - 1))

        def bank_of(s, kind, i=0):
            if isinstance(s, int) and (kind, i) in LAST_BANKS.get(s, {}):
                return LAST_BANKS[s][kind, i][0]
            return psM[:, :]

        def misc_free(e, s, on, job):
            if isinstance(s, int) and job in LAST_BANKS.get(s, {}):
                wait(e, *LAST_BANKS[s][job][1])
                return
            order = misc_users(s, on)
            i = [o[0] for o in order].index(job)
            if i:
                wait(e, order[i - 1][1], order[i - 1][2])
                return
            if isinstance(s, int):
                before = s - 1
                while before >= -2 and not misc_users(before, on_of(before)):
                    before -= 1
                if before < -2:
                    return
                last = misc_users(before, on_of(before))[-1]
            else:
                last = misc_users(s - 1, on)[-1]
            wait(e, last[1], last[2])

        @block.sync
        def _(sp):
            def store_part(j, p, s):
                name = "qk"[j] + ("_hi", "_mid", "_lo")[p]
                wait(sp, name, s + 3)
                sp.dma_start(scratch[j, p].rearrange("e d g t -> g (e d) t"), parts[:, j, p])\
                  .then_inc(part_out[j][p], 16)

            def load_queries(run, s):
                first, n, part = run
                sp.wait_ge(part_out[0][part], 16 * (s + 2))
                for e in range(2):
                    r = STACK * e + HS * first
                    src = scratch[0, part:part + 1, e].rearrange("p d g t -> p d (g t)")
                    sp.dma_start(Qs[(s + 1) % 2][r:r + HS * n, :, :], src.to_broadcast([n, HS, NH // 2 * T]))\
                      .then_inc(S["stacks_in"], 16)

            def load_keys(run, s):
                first, n, _ = run
                for p in range(n):
                    sp.wait_ge(part_out[1][p], 16 * (s + 2))
                for e in range(2):
                    r = STACK * e + HS * first
                    sp.dma_start(Ks[(s + 1) % 2][r:r + HS * n, e * NH // 2:(e + 1) * NH // 2, :],
                                 scratch[1, 0:n, e].rearrange("p d g t -> p d (g t)"))\
                      .then_inc(S["stacks_in"], 16)

            def store_parts(s):
                wait(sp, "stacks_in", LOADS * (s + 2))
                for j in range(2):
                    for p in range(PARTS):
                        store_part(j, p, s)

            def load_stacks(s):
                wait(sp, "b_ready", B_ITEMS * NG * s)
                if s < 1:
                    wait(sp, "q_zero", s + 2)
                    wait(sp, "ks1_zero", 1)
                for run in RUNS:
                    load_queries(run, s)
                for run in reversed(RUNS):
                    load_keys(run, s)

            sp.dma_start(X[:, 0], x[0].rearrange("(t p) c -> p t c", p=128)).then_inc(x_in[0], 16)
            sp.dma_start(W64[:, :], w64).then_inc(S["w64_in"], 16)
            for b in range(1, 2):
                sp.dma_start(X[:, b], x[b].rearrange("(t p) c -> p t c", p=128)).then_inc(x_in[b], 16)
            sp.dma_start(boR[:, :], bo).then_inc(S["bo_in"], 16)
            store_part(0, 0, -2)
            store_part(0, 1, -2)
            store_part(1, 0, -2)
            store_part(0, 2, -2)
            wait(sp, "q_zero", 1)
            load_queries(RUNS[0], -1)
            store_part(1, 1, -2)
            load_queries(RUNS[1], -1)
            store_part(1, 2, -2)
            load_queries(RUNS[2], -1)
            wait(sp, "ks0_zero", 1)
            for run in reversed(RUNS):
                load_keys(run, -1)
            for i in range(2):
                wait(sp, f"ks{i}_zero", 1)
                sp.dma_start(Ks[i][MAX_ROW:MAX_ROW + PARTS * HG, :, :], sel.bitcast(bf16)).then_inc(S["sel_in"], 16)
            for b in range(2, B):
                sp.dma_start(X[:, b], x[b].rearrange("(t p) c -> p t c", p=128)).then_inc(x_in[b], 16)

            def job(s, par, on):
                for k in range(NG):
                    if k == 0 and on["v"] and s >= 0:
                        load_stacks(s)
                    if k == 3 and on["pre"]:
                        store_parts(s)

            slots(sp, job)
            for b in LAST_ORDER:
                for name, share in (("pool_ready", POOL_SHARE), ("dve_ready", DVE_SHARE)):
                    mine = [n for n, (of, _) in enumerate(share) if of == b]
                    if mine:
                        wait(sp, name, mine[-1] + 1)
                sp.dma_start(out[b].rearrange("(t p) c -> p t c", p=128), X[:, b]).then_inc(S["out_done"], 16)
            sp.wait_ge(S["out_done"], 16 * B)

        @block.gpsimd
        def _(pool):
            def rest_part(j, name, s):
                wait(pool, name + "_copied", s + 2)
                wait(pool, name + "_hi", s + 3)
                pool.tensor_tensor(rest[:, j], rest[:, j], parts[:, j, 0], ALU.subtract)\
                    .then_inc(S[name + "_rest"], 1)

            def low_half(name, full, count):
                wait(pool, name + "_high", count)
                pool.tensor_tensor(halves[name][1][:, :], full[:, :], halves[name][0][:, :].bitcast(f32),
                    ALU.subtract)\
                    .then_inc(S[name + "_low"], 1)

            def low_part(j, name, s):
                wait(pool, name + "_mid", s + 3)
                pool.tensor_tensor(parts[:, j, 2], rest[:, j], parts[:, j, 1], ALU.subtract)\
                    .then_inc(S[name + "_lo"], 1)

            c = S["consts"]
            pool.memset(ident[:, :], 0.0).then_inc(c, 1)
            pool.memset(identb[:, :], 0.0).then_inc(c, 1)
            pool.memset(causal[:, :], 0.0).then_inc(c, 1)
            pool.memset(causalT[:, :], 0.0).then_inc(c, 1)
            pool.memset(expo[:, :], -0.5).then_inc(c, 1)
            pool.memset(onesR[:, :], 1.0).then_inc(c, 1)
            pool.wait_ge(c, 6)
            for m in (ident, identb):
                pool.affine_select(out=m[:, :], in_=m[:, :], compare_op=ALU.not_equal, fill=1.0, base=0,
                                   pattern=[[-1, 128]], channel_multiplier=1).then_inc(c, 1)
            pool.affine_select(out=causal[:, :], in_=causal[:, :], compare_op=ALU.is_ge, fill=MASKED, base=0,
                               pattern=[[-1, 128]], channel_multiplier=1).then_inc(c, 1)
            pool.affine_select(out=causalT[:, :], in_=causalT[:, :], compare_op=ALU.is_ge, fill=MASKED, base=0,
                               pattern=[[1, 128]], channel_multiplier=-1).then_inc(c, 1)
            pool.memset(Qs[0][:, :, :].bitcast(f32), 0.0).then_inc(S["q_zero"], 1)
            wait(pool, "var_done", 1)
            pool.tensor_tensor(rstd[:, 0], varp[:, 0], expo[:, :], ALU.pow).then_inc(S["rstd_done"], 1)
            pool.memset(Ks[0][:, :, :].bitcast(f32), 0.0).then_inc(S["ks0_zero"], 1)
            pool.memset(Ks[1][:, :, :].bitcast(f32), 0.0).then_inc(S["ks1_zero"], 1)
            low_part(0, "q", -2)
            low_part(1, "k", -2)
            def power(j, done):
                pool.tensor_tensor(rstd[:, j], varp[:, j], expo[:, :], ALU.pow).then_inc(S[done], 1)

            def centre(j, b, two):
                wait(pool, "h2_turned" if two else "h_turned", b)
                pool.tensor_tensor(xn[:, j], X[:, b], mv[:, j, :, 0:1].to_broadcast([128, NT, C]), ALU.subtract)\
                    .then_inc(S[f"centred{two}"], 1)
                wait(pool, f"rstd{two}_done", b + 1)
                wait(pool, f"centred{two}", b + 1 if two else b)
                pool.tensor_tensor(xn[:, j], xn[:, j], rstd[:, j].unsqueeze(2).to_broadcast([128, NT, C]), ALU.mult)\
                    .then_inc(S[f"xn{two}_done"], 1)

            def job(s, par, on):
                b = s - 1

                def gated():
                    wait(pool, "gate_done", 4)
                    for t in range(NT):
                        wait(pool, "y_scaled", NY * b + t // YT + 1)
                        pool.tensor_tensor(y[:, t], y[:, t], gate[:, b, 0, :], ALU.mult).then_inc(S["ga_done"], 1)
                        if t:
                            add(t - 1)
                    add(NT - 1)

                def add(t):
                    wait(pool, "ga_done", NT * b + t + 1)
                    pool.tensor_tensor(X[:, b, t], X[:, b, t], y[:, t], ALU.add).then_inc(S["x1_done"], 1)

                for k in range(NG):
                    if k == 0 and on["pre"]:
                        wait(pool, "var_done", s + 3)
                        power(0, "rstd_done")
                        centre(0, s + 2, "")
                    if k == 0 and on["post2"] and s < B + 1:
                        low_half("s", sT, s)
                    if k == 1 and on["post"]:
                        gated()
                    if k == 0 and s == -1:
                        pool.memset(Qs[1][:, :, :].bitcast(f32), 0.0).then_inc(S["q_zero"], 1)
                    if k == 2 and on["pre"]:
                        low_half("h", hT, s + 2)
                    if k == 2 and on["post"]:
                        wait(pool, "var2_done", s)
                        power(1, "rstd2_done")
                        if s < B:
                            centre(1, s - 1, "2")
                    if k == 2 and on["pre"]:
                        rest_part(0, "q", s)
                        rest_part(1, "k", s)
                    if k == 3 and on["post"] and s < B:
                        low_half("h2", h2T, s)
                    if k == 3 and on["pre"]:
                        low_part(0, "q", s)
                        low_part(1, "k", s)

            slots(pool, job)
            for n, (b, tiles) in enumerate(POOL_SHARE):
                pool.wait_ge(S["tanh_done"], LAST_ORDER.index(b) + 1)
                gb = gate[:, b, 1, :].unsqueeze(1).to_broadcast([128, len(range(NT)[tiles]), C])
                pool.tensor_tensor(zt[b][:, tiles], zt[b][:, tiles], gb, ALU.mult).then_inc(S["zgate_pool"], 1)
                pool.wait_ge(S["zgate_pool"], n + 1)
                pool.tensor_tensor(X[:, b, tiles], X[:, b, tiles], zt[b][:, tiles], ALU.add)\
                    .then_inc(S["pool_ready"], 1)

        @block.scalar
        def _(act):
            for name, first, last in (("w_a", "W_uk", "W_oT"), ("w_mod", "wmod", "cT"), ("w_rest", "wfT", "ucT"),
                                      ("w_rest", "woT", "in_c")):
                act.dma_start(columns(first, last), w128[:, at[first][0]:at[last][1]]).then_inc(S[name], 16)
            act.wait_ge(S["w_mod"], 16)
            act.activation(silu_t[:, :], w("cT"), ACT.Tanh, scale=0.5).then_inc(S["th_done"], 1)

            def turned(dst, made, copied, scale, shift, b, count, bank, high=None):
                wait(act, made, count)
                wait(act, "mod_done", scale + 1)
                act.activation(dst[:, :], bank, ACT.Identity, bias=modc[:, shift, bass.ds(b, 1)],
                               scale=modc[:, scale, bass.ds(b, 1)]).then_inc(S[copied], 1)
                if high:
                    act.activation(halves[high][0][:, :], bank, ACT.Identity, bias=modc[:, shift, bass.ds(b, 1)],
                                   scale=modc[:, scale, bass.ds(b, 1)]).then_inc(S[high + "_high"], 1)

            def high_part(j, name, s, bank=psM[:, :]):
                wait(act, name + "_made", s + 3)
                if s >= -1:
                    for p in range(PARTS):
                        act.wait_ge(part_out[j][p], 16 * (s + 2))
                act.activation(parts[:, j, 0], bank, ACT.Copy).then_inc(S[name + "_hi"], 1)
                if s >= -1:
                    wait(act, name + "_lo", s + 2)
                    act.activation(rest[:, j], bank, ACT.Copy).then_inc(S[name + "_copied"], 1)

            def mid_part(j, name, s):
                wait(act, name + "_rest", s + 3)
                act.activation(parts[:, j, 1], rest[:, j], ACT.Copy).then_inc(S[name + "_mid"], 1)

            def gate_act(dst, name, s, bias, scale):
                wait(act, name + "_made", s)
                wait(act, "s_done", s - 1)
                act.activation(dst[:, :], bank_of(s, name), ACT.Tanh, bias=bias, scale=scale)\
                   .then_inc(S[name + "_act"], 1)

            def y_copy(ypar, n, b):
                wait(act, "pv_done", NG * b + min(SET * (n + 1), NG))
                wait(act, "y_turned", NY * (b - 1))
                act.activation(Y[ypar][:, n, :], psY[:, :], ACT.Copy).then_inc(S["y_copied"], 1)

            def job(s, par, on):
                for k in range(NG):
                    for i in range(B_ITEMS):
                        if on["b"]:
                            G = 4 * s + k
                            slot = (k + i) % 2
                            wait(act, "b_ready", B_ITEMS * G + i + 1)
                            if i == 0:
                                wait(act, "pv_done", G - 1)
                            act.activation(P[k % 2][:, 2 * i:2 * i + 2, :], psB[:, 2 * slot:2 * slot + 2, :],
                                           ACT.Exp, scale=SCALE).then_inc(S["exp_done"], 1)
                        if (k, i) == (3, 4) and on["b"]:
                            y_copy(par, 0, s)
                        if (k, i) == (0, 4) and on["post"] and s < B:
                            y_copy(1 - par, 1, s - 1)
                        if i == M_AT[k] and on["m"][k]:
                            G, gk = NG * s + k + 1, (k + 1) % NG
                            rows = psM[MAX_ROW:MAX_ROW + PARTS * HG, 0:T // 2].bitcast(bf16)
                            wait(act, "m_turned", G + 1)
                            act.activation(Qs[par if k < NG - 1 else 1 - par]
                                           [MAX_ROW:MAX_ROW + PARTS * HG, 2 * gk:2 * gk + 2, :],
                                           rows.unsqueeze(1).to_broadcast([PARTS * HG, 2, T]), ACT.Copy)\
                               .then_inc(S["m_copied"], 1)
                        if (k, i) == (0, 3) and s == B:
                            y_copy(1 - par, 1, s - 1)
                        if (k, i) == (0, 3) and on["post2"]:
                            wait(act, "z_made", s - 1)
                            act.activation(ZX[:, s - 2], bank_of(s, "z").rearrange("p (t c) -> p t c", t=NT), ACT.Copy)\
                               .then_inc(S["z_copied"], 1)
                        if (k, i) == (0, 4) and on["post2"] and s < B + 1:
                            wait(act, "s_done", s - 1)
                            act.activation(halves["s"][0][:, :], sT[:, :], ACT.Copy).then_inc(S["s_high"], 1)
                        if (k, i) == (0, 4) and on["v"]:
                            wait(act, "v_made", s + 2)
                            wait(act, "pv_done", 4 * s)
                            if s < 1:
                                act.wait_ge(S["va_zero"], 2 * (s + 2))
                            act.activation(Va[1 - par][:, :, 0:NH, V_AT:V_AT + HS],
                                           psM[:, :].rearrange("p (t h d) -> p t h d", t=NT, d=HS), ACT.Copy)\
                               .then_inc(S["v_copied"], 1)
                        if on["post"] and s < B and (k, i) in ((1, 0), (1, 1)):
                            n = NY * (s - 1) + i + 1
                            wait(act, "y_turned", n)
                            wait(act, "s_done", s - 1)
                            wait(act, "y_scaled", n - NY)
                            act.activation(turned_out[i][:, :], psM[:, :], ACT.Copy).then_inc(S["yt_copied"], 1)
                        if (k, i) == (1, 3) and on["pre"]:
                            turned(hT, "h_turned", "h_copied", 1, 0, s + 2, s + 3, psM[:, :], "h")
                        if (k, i) == Q_STEP[s == -1] and on["pre"]:
                            high_part(0, "q", s)
                        if (k, i) == K_STEP[s == -1] and on["pre"]:
                            high_part(1, "k", s)
                        if (k, i) == (3, 0) and on["pre"]:
                            mid_part(0, "q", s)
                        if (k, i) == (3, 2) and on["pre"]:
                            mid_part(1, "k", s)
                        if (k, i) == (2, 4) and on["post"]:
                            turned(h2T, "h2_turned", "h2_copied", 3, 2, s - 1, s, bank_of(s, "h2"), "h2")
                        if (k, i) == (3, 1) and on["post"]:
                            gate_act(gf, "f", s, half_b[:, 0:1], 0.5)
                        if (k, i) == (3, 3) and on["post"]:
                            gate_act(gi, "i", s, half_b[:, 1:2], 0.5)
                        if (k, i) == (3, 4) and on["post"]:
                            gate_act(gg, "g", s, w("bc"), 1.0)

            turned(hT, "h_turned", "h_copied", 1, 0, 0, 1, psB[:, 0, :])
            high_part(0, "q", -2, psB[:, 0, :])
            high_part(1, "k", -2, psB[:, 1, :])
            for n, bank in enumerate((2, 3, 0, 1)):
                act.wait_ge(S["gate_made"], n + 1)
                act.activation(gate[:, 2 * bank:2 * bank + 2],
                               psB[:, bank, :].rearrange("p (b j c) -> p b j c", b=2, j=2), ACT.Copy)\
                   .then_inc(S["gate_done"], 1)
            slots(act, job)
            for n, b in enumerate(LAST_ORDER):
                act.wait_ge(S["zsum_done"], n + 1)
                act.activation(zt[b], ZX[:, b], ACT.Tanh).then_inc(S["tanh_done"], 1)

        @block.vector
        def _(dve):
            sv = [0]

            def done_setup(ins):
                sv[0] += 1
                ins.then_inc(S["setup_v"], 1)
                return sv[0]

            def norm_stats(j, b, two, tiles=range(NT)):
                if not two and tiles[0] == 0:
                    dve.wait_ge(x_in[b], 16)
                for t in tiles:
                    if two:
                        wait(dve, "x1_done", NT * b + t + 1)
                    last = dve.bn_stats(stat[:, j, t, :], X[:, b, t, :])
                if tiles[-1] == NT - 1:
                    last.then_inc(S[f"stat{two}_done"], 1)

            def norm_mean(j, b, two):
                wait(dve, f"stat{two}_done", 2 * b + 1)
                for t in range(NT):
                    last = dve.bn_aggr(mv[:, j, t, :], stat[:, j, t, :])
                last.then_inc(S[f"stat{two}_done"], 1)

            def norm_var(j, two, count):
                wait(dve, f"stat{two}_done", 2 * count)
                dve.tensor_scalar(varp[:, j], mv[:, j, :, 1], EPS, None, ALU.add).then_inc(S[f"var{two}_done"], 1)

            def norm_apply(j, b, two, tiles=range(NT)):
                wait(dve, f"rstd{two}_done", b + 1)
                for t in tiles:
                    last = dve.tensor_scalar(xn[:, j, t], X[:, b, t, :], mv[:, j, t, 0:1], rstd[:, j, t:t + 1],
                                             ALU.subtract, ALU.mult)
                if tiles[-1] == NT - 1:
                    last.then_inc(S[f"xn{two}_done"], 1)

            def reduce_item(G, kk, i):
                wait(dve, "a_ready", A_ITEMS * G + i + 1)
                bank = psA[:, i % 2, :].rearrange("p (n c) -> p n c", n=4)
                d = bm[:, kk % 2]

                def diagonal(n, o):
                    return dve.tensor_tensor_reduce(bank[:, n], bank[:, n], causal[:, :], 1.0, LOWEST,
                                                    ALU.add, ALU.max, o)

                if G < LEAD:
                    if i < 4:
                        o = d[:, i, 3, :]
                    elif i < 8:
                        o = d[:, i - 4].rearrange("p a b -> p (a b)")[:, 1:5]
                    else:
                        o = d[:, 2 * (i - 8):2 * (i - 8) + 2, 2, 0:2]
                    last = dve.tensor_reduce(o, bank, AX.X, ALU.max)
                elif i < 4:
                    dve.tensor_reduce(d[:, i, 3, 0:3], bank[:, 0:3], AX.X, ALU.max)
                    last = diagonal(3, d[:, i, 3, 3:4])
                elif i < 8:
                    o = d[:, i - 4].rearrange("p a b -> p (a b)")
                    dve.tensor_reduce(o[:, 1:3], bank[:, 0:2], AX.X, ALU.max)
                    diagonal(2, o[:, 3:4])
                    last = diagonal(3, o[:, 4:5])
                else:
                    h = 2 * (i - 8)
                    dve.tensor_reduce(d[:, h:h + 2, 2, 0], bank[:, 0:4:2], AX.X, ALU.max)
                    diagonal(1, d[:, h, 2, 1:2])
                    last = diagonal(3, d[:, h + 1, 2, 1:2])
                last.then_inc(S["a_reduced"], 1)

            def finish_max(G, kk):
                wait(dve, "a_reduced", A_ITEMS * (G + 1))
                dve.tensor_reduce(nm[:, kk % 2], bm[:, kk % 2], AX.X, ALU.max, negate=True)\
                   .then_inc(S["nm_done"], 1)

            def part1(G, kk):
                wait(dve, "nm_done", G + 1)
                wait(dve, "m_turned", G - 1)
                dve.tensor_copy(nparts[:, kk % 2, :, 0, :], nm[:, kk % 2].rearrange("p h t -> p t h"))\
                   .then_inc(S["n_part"], 1)

            def part1r(G, kk):
                wait(dve, "n_part", 2 * G + 1)
                dve.tensor_tensor(nr[:, kk % 2], nm[:, kk % 2],
                                  nparts[:, kk % 2, :, 0, :].rearrange("p t h -> p h t"), ALU.subtract)\
                   .then_inc(S["nr_done"], 1)

            def part2(G, kk):
                wait(dve, "nr_done", G + 1)
                dve.tensor_copy(nparts[:, kk % 2, :, 1, :], nr[:, kk % 2].rearrange("p h t -> p t h"))\
                   .then_inc(S["n_part"], 1)

            def part3(G, kk):
                wait(dve, "n_part", 2 * G + 2)
                dve.tensor_tensor(nparts[:, kk % 2, :, 2, :], nr[:, kk % 2].rearrange("p h t -> p t h"),
                                  nparts[:, kk % 2, :, 1, :], ALU.subtract).then_inc(S["n_ready"], 1)

            small = [finish_max, part1, part1r, part2, part3]

            def high_half(name, full):
                dve.tensor_copy(halves[name][0][:, :], full[:, :]).then_inc(S[name + "_high"], 1)

            def low_half(name, full, count):
                wait(dve, name + "_high", count)
                dve.tensor_tensor(halves[name][1][:, :], full[:, :], halves[name][0][:, :].bitcast(f32),
                    ALU.subtract)\
                   .then_inc(S[name + "_low"], 1)

            def turned_y(bank):
                tiles = bank.rearrange("p (t n c) -> p t n c", t=YT, n=SETS)
                for m in range(SETS):
                    g = slice(SET * m, min(SET * (m + 1), NG))
                    yield tiles[:, :, m].rearrange("p t (h r) -> p t h r", r=32)[:, :, :, 0:HV * (g.stop - g.start)]\
                        .rearrange("p t h (g d) -> p t h g d", d=HV), g

            def invert_y(n, b, bank):
                wait(dve, "yt_copied" if b < B - 1 else "y_turned", NY * b + n + 1)
                for heads, g in turned_y(bank):
                    last = dve.reciprocal(rden[:, YT * n:YT * n + YT, :, g], heads[:, :, :, :, HS])
                last.then_inc(S["r_done"], 1)

            def scale_y(n, b, bank):
                y_ = y[:, :, :].rearrange("p t (g h d) -> p t h g d", g=NG, d=HS)
                wait(dve, "r_done", NY * b + n + 1)
                if n == 0:
                    wait(dve, "x1_done", NT * b)
                for i in range(YT):
                    t = YT * n + i
                    for heads, g in turned_y(bank):
                        last = dve.tensor_tensor(y_[:, t, :, g], heads[:, i, :, :, 0:HS],
                                                 rden[:, t, :, g].unsqueeze(3)
                                                 .to_broadcast([128, HG, g.stop - g.start, HS]), ALU.mult)
                last.then_inc(S["y_scaled"], 1)

            def job(s, par, on):
                for k in range(NG):
                    for i in range(A_ITEMS):
                        def split(n):
                            if on["m"][k]:
                                small[n](4 * s + k + LEAD - 1, k + 1)

                        if i == 0:
                            split(0)
                        if on["a"][k]:
                            reduce_item(4 * s + k + LEAD, k, i)
                        if i < 4:
                            split(i + 1)
                        if (k, i) == (0, 3) and on["post2"]:
                            wait(dve, "g_act", s - 1)
                            wait(dve, "i_act", s - 1)
                            dve.scalar_tensor_tensor(out=gi[:, :], in0=gi[:, :], scalar=1.0, in1=gg[:, :],
                                                     op0=ALU.add, op1=ALU.mult).then_inc(S["v_done"], 1)
                        if (k, i) == (0, 6) and on["post2"]:
                            wait(dve, "v_done", s - 1)
                            wait(dve, "u_done", s - 1)
                            dve.scalar_tensor_tensor(out=sT[:, :], in0=gf[:, :], scalar=0.5, in1=gi[:, :],
                                                     op0=ALU.mult, op1=ALU.add).then_inc(S["s_done"], 1)
                        if (k, i) == (3, 0) and s == B:
                            low_half("h2", h2T, s)
                        if s + 3 < B:
                            if (k, i) in ((3, 6), (3, 7)):
                                norm_stats(0, s + 3, "", range(2 * (i - 6), 2 * (i - 6) + 2))
                            if (k, i) == (3, 8):
                                wait(dve, "centred", s + 2)
                                norm_mean(0, s + 3, "")
                            if (k, i) == (3, 9):
                                norm_var(0, "", s + 4)
                        if on["post"]:
                            if k == 1 and 2 <= i < 7 and i != 4:
                                n = i // 4
                                source = turned_out[n][:, :] if s < B else bank_of(s, "y", n)
                                (invert_y if i in (2, 5) else scale_y)(n, s - 1, source)
                            if (k, i) == (1, 9):
                                norm_stats(1, s - 1, "2", range(0, 2))
                            if (k, i) == (2, 1):
                                norm_stats(1, s - 1, "2", range(2, NT))
                            if (k, i) == (2, 2):
                                norm_mean(1, s - 1, "2")
                            if (k, i) == (2, 3):
                                norm_var(1, "2", s)
                            if s == B and (k, i) in ((2, 6), (2, 8)):
                                norm_apply(1, s - 1, "2", range(i - 6, i - 4))
                        if (k, i) == (3, 5) and on["post"]:
                            wait(dve, "f_act", s)
                            dve.scalar_tensor_tensor(out=gf[:, :], in0=gf[:, :], scalar=1.0, in1=sT[:, :],
                                                     op0=ALU.add, op1=ALU.mult).then_inc(S["u_done"], 1)

            for j in range(2):
                done_setup(dve.memset(bm[:, j], LOWEST))
            zeroed = done_setup(dve.memset(sT[:, :], 0.0))
            norm_stats(0, 0, "")
            norm_mean(0, 0, "")
            norm_var(0, "", 1)
            dve.wait_ge(S["th_done"], 1)
            dve.scalar_tensor_tensor(out=silu[:, :], in0=silu_t[:, :], scalar=1.0, in1=w("cT"),
                                     op0=ALU.add, op1=ALU.mult).then_inc(S["silu_done"], 1)
            dve.wait_ge(S["setup_mm"], 1)
            done_setup(dve.tensor_copy(AT[:, :], psA[:, 1, 0:C]))
            assert done_setup(dve.tensor_copy(VE[:, :], psY[0:KVL, 0:C])) == AT_VE
            norm_apply(0, 0, "")
            assert done_setup(dve.tensor_copy(WQ[:, :], psA[:, 0, 0:C])) == AT_VE_WQ

            def modulation(half):
                dve.wait_ge(S["mod_made"], half + 1)
                dve.tensor_scalar(modc[:, 2 * half], mod[:, 3 * half], 0.5, None, ALU.mult)\
                   .then_inc(S["mod_done"], 1)
                dve.tensor_scalar(modc[:, 2 * half + 1], mod[:, 3 * half + 1], 0.5, 1.0, ALU.mult, ALU.add)\
                   .then_inc(S["mod_done"], 1)

            modulation(0)
            dve.wait_ge(S["setup_mm"], 2)
            assert done_setup(dve.tensor_copy(KE[:, :], psB[0:KVL, 2, 0:C])) == AT_VE_WQ_KE
            done_setup(dve.tensor_copy(WV[:, :], psB[:, 3, 0:C]))
            dve.wait_ge(S["setup_mm"], 3)
            assert done_setup(dve.tensor_copy(WK[:, :], psB[:, 1, 0:C])) == ALL_WEIGHTS
            for j, name in enumerate("qk"):
                wait(dve, name + "_hi", 1)
                dve.tensor_tensor(rest[:, j], psB[:, j, :], parts[:, j, 0], ALU.subtract)\
                   .then_inc(S[name + "_rest"], 1)
                wait(dve, name + "_rest", 1)
                dve.tensor_copy(parts[:, j, 1], rest[:, j]).then_inc(S[name + "_mid"], 1)
            modulation(1)
            raw = done_setup(dve.tensor_scalar(gcol[:, :, :], mod[:, 2:6:3], 0.5, None, ALU.mult))
            dve.wait_ge(S["setup_v"], raw)
            done_setup(dve.tensor_scalar(gsign[:, :, :], gcol[:, :, :], 0.0, 2.0, ALU.is_ge, ALU.mult))
            n = done_setup(dve.scalar_tensor_tensor(out=gabs[:, :, :], in0=gcol[:, :, :], scalar=-1.0,
                                                    in1=gcol[:, :, :], op0=ALU.mult, op1=ALU.max))
            dve.wait_ge(S["setup_v"], n)
            n = done_setup(dve.tensor_scalar(gabs[:, :, :], gabs[:, :, :], 0.25, None, ALU.max))
            dve.wait_ge(S["setup_v"], n)
            dve.scalar_tensor_tensor(out=gcol[:, :, :], in0=gsign[:, :, :], scalar=-1.0, in1=gabs[:, :, :],
                                     op0=ALU.add, op1=ALU.mult).then_inc(S["gcol_done"], 1)
            norm_stats(0, 1, "")
            norm_mean(0, 1, "")
            norm_var(0, "", 2)
            dve.wait_ge(S["w_rest"], 32)
            dve.wait_ge(S["setup_v"], zeroed)
            dve.tensor_scalar(sT[:, :], sT[:, :], w("in_c"), 2.0, ALU.add, ALU.mult).then_inc(S["state_set"], 1)
            dve.tensor_scalar(half_b[:, :], columns("bf", "bi"), 0.5, None, ALU.mult)\
               .then_inc(S["state_set"], 1)
            u3 = columns("ufT", "ucT")
            dve.tensor_scalar(u3, u3, 0.5, None, ALU.mult).then_inc(S["state_set"], 1)
            dve.tensor_scalar(w("uoT"), w("uoT"), 0.5, None, ALU.mult).then_inc(S["state_set"], 1)
            dve.wait_ge(S["k_made"], 1)
            for j, weights in enumerate((WQ, WK)):
                dve.tensor_copy(QK_high[:, j], weights[:, :]).then_inc(S["qk_high"], 1)
            dve.wait_ge(S["state_set"], 4)
            high_half("s", sT)
            gates_w = columns("wfT", "ucT")
            dve.tensor_copy(W_high[:, :], gates_w).then_inc(S["w_high"], 1)
            dve.wait_ge(S["qk_high"], 2)
            for j, weights in enumerate((WQ, WK)):
                dve.tensor_tensor(QK_low[:, j], weights[:, :], QK_high[:, j].bitcast(f32), ALU.subtract).then_inc(S["qk_split"], 1)
            low_half("s", sT, 1)
            dve.wait_ge(S["w_high"], 1)
            dve.tensor_tensor(W_low[:, :], gates_w, W_high[:, :].bitcast(f32), ALU.subtract).then_inc(S["w_split"], 1)
            for i in range(2):
                dve.memset(Va[i][:, :, :, :], 0.0).then_inc(S["va_zero"], 1)
                dve.wait_ge(S["va_zero"], 2 * i + 1)
                dve.memset(Va[i][:, :, 0:NH, V_AT + HS:V_AT + HV], 1.0).then_inc(S["va_zero"], 1)

            slots(dve, job)
            dve.wait_ge(S["z_copied"], B)
            dve.wait_ge(S["cu_made"], 1)
            cu = psB[:, 1, :].rearrange("p (t c) -> p t c", t=NT)

            def finish(n):
                b, tiles = DVE_SHARE[n]
                dve.wait_ge(S["tanh_done"], LAST_ORDER.index(b) + 1)
                gb = gate[:, b, 1, :].unsqueeze(1).to_broadcast([128, len(range(NT)[tiles]), C])
                dve.tensor_tensor(zt[b][:, tiles], zt[b][:, tiles], gb, ALU.mult).then_inc(S["zgate_done"], 1)
                dve.wait_ge(S["zgate_done"], n + 1)
                dve.tensor_tensor(X[:, b, tiles], X[:, b, tiles], zt[b][:, tiles], ALU.add)\
                   .then_inc(S["dve_ready"], 1)

            for n, b in enumerate(LAST_ORDER):
                dve.tensor_tensor(ZX[:, b], ZX[:, b], cu, ALU.add).then_inc(S["zsum_done"], 1)
                if n >= 3 and n % 2:
                    finish(n // 2 - 1)
            for n in range(B // 2 - 1, len(DVE_SHARE)):
                finish(n)

        @block.tensor
        def _(pe):
            def mm(o, l, r, start=True, stop=True):
                return pe.matmul(o, l, r, start=start, stop=stop)

            def product(o, high, low, name, start=True, stop=True):
                x_high, x_low = (x_[:, :] for x_ in halves[name])
                mm(o, high, x_high, start, False)
                mm(o, low, x_high, False, False)
                return mm(o, high, x_low, False, stop)

            pe.wait_ge(S["w64_in"], 16)
            pe.wait_ge(S["w_a"], 16)
            mm(psA[:, 0, 0:C], W_dq, W_uqT)
            mm(psA[:, 1, 0:C], W_uqT, W_dq)
            mm(psY[0:KVL, 0:C], w("W_uv"), w("W_oT")).then_inc(S["setup_mm"], 1)
            wm = w("wmod").rearrange("p (j c) -> p j c", j=6)

            def modulate(js):
                for j in js:
                    last = mm(mod[:, j], wm[:, j], silu[:, :])
                last.then_inc(S["mod_made"], 1)

            pe.wait_ge(S["silu_done"], 1)
            modulate((0, 1))
            pe.wait_ge(S["setup_v"], AT_VE)
            mm(psB[0:KVL, 2, 0:C], w("W_uk"), AT[:, :])
            mm(psB[:, 3, 0:C], W_dkv, VE[:, :]).then_inc(S["setup_mm"], 1)
            pe.wait_ge(S["consts"], 10)
            pe.wait_ge(S["xn_done"], 1)
            for t in range(NT):
                last = pe.transpose(psB[:, 0, t * 128:(t + 1) * 128], xn[:, 0, t], ident[:, :])
            last.then_inc(S["h_turned"], 1)
            pe.wait_ge(S["setup_v"], AT_VE_WQ_KE)
            mm(psB[:, 1, 0:C], W_dkv, KE[:, :]).then_inc(S["setup_mm"], 1)
            pe.wait_ge(S["h_copied"], 1)
            mm(psB[:, 0, :], WQ[:, :], hT[:, :]).then_inc(S["q_made"], 1)
            pe.wait_ge(S["setup_v"], ALL_WEIGHTS)
            mm(psB[:, 1, :], WK[:, :], hT[:, :]).then_inc(S["k_made"], 1)
            modulate((3, 4, 2, 5))
            pe.wait_ge(S["gcol_done"], 1)
            for bank in (2, 3, 0, 1):
                if bank == 0:
                    pe.wait_ge(S["k_rest"], 1)
                for n in range(4):
                    b, j = 2 * bank + n // 2, n % 2
                    last = mm(psB[:, bank, n * 128:(n + 1) * 128],
                              gcol[:, j, b:b + 1].to_broadcast([128, 128]), ident[:, :])
                last.then_inc(S["gate_made"], 1)

            def scores_max(G, gk, bpar, i):
                wait(pe, "a_reduced", A_ITEMS * G + i - 1)
                q_, k_ = Qs[bpar], Ks[bpar]
                bank = psA[:, i % 2, :]

                def tile(h, t, c0):
                    n_ = (t + 1) * 128
                    hh = gk * HG + h
                    last = mm(bank[:, c0:c0 + n_], q_[0:MAX_ROW, hh // 2, t * 128:(t + 1) * 128],
                              k_[0:MAX_ROW, key_at(hh), 0:n_], True, G >= LEAD)
                    if G < LEAD:
                        last = mm(bank[:, c0 + n_ - 128:c0 + n_], identb[:, :], causal[:, :], False, True)
                    return last

                if i < 4:
                    last = tile(i, 3, 0)
                elif i < 8:
                    tile(i - 4, 2, 0)
                    last = tile(i - 4, 0, 384)
                else:
                    tile(2 * (i - 8), 1, 0)
                    last = tile(2 * (i - 8) + 1, 1, 256)
                last.then_inc(S["a_ready"], 1)

            def scores(G, k, bpar, i):
                wait(pe, "exp_done", B_ITEMS * G + i - 1)
                q_, k_ = Qs[bpar], Ks[bpar]
                slot = (k + i) % 2

                def tile(h, kb, bank, c0):
                    hh = k * HG + h
                    mm(psB[:, 2 * slot + bank, c0:c0 + T - kb * 128],
                       k_[:, key_at(hh), kb * 128:(kb + 1) * 128], q_[:, hh // 2, kb * 128:T], c0 == 0, False)

                def mask(bank, step, n):
                    o = psB[:, 2 * slot + bank, :].rearrange("p (n c) -> p n c", n=4)[:, 0:step * (n - 1) + 1:step]
                    return mm(o, identb[:, :], causalT[:, :].unsqueeze(1).to_broadcast([128, n, 128]), False, True)

                for bank in range(2):
                    if i < 2:
                        tile(2 * i + bank, 0, bank, 0)
                        last = mask(bank, 1, 1)
                    elif i < 4:
                        h = 2 * (i - 2) + bank
                        tile(h, 1, bank, 0)
                        tile(h, 3, bank, 384)
                        last = mask(bank, 3, 2)
                    else:
                        tile(2 * bank, 2, bank, 0)
                        tile(2 * bank + 1, 2, bank, 256)
                        last = mask(bank, 2, 2)
                last.then_inc(S["b_ready"], 1)

            def p_view(p_, h, kb):
                if kb == 0:
                    return p_[:, h, 0:512]
                if kb == 1:
                    return p_[:, 4 + h, 0:384]
                if kb == 3:
                    return p_[:, 4 + h, 384:512]
                return p_[:, 8 + h // 2, (h % 2) * 256:(h % 2) * 256 + 256]

            def values(G, gk, bpar, kb):
                n = gk // SET
                wait(pe, "exp_done", B_ITEMS * G + (2, 4, 5, 5)[kb])
                if kb == 0:
                    if gk % SET == 0:
                        wait(pe, "y_copied", SETS * (G // NG) + n)
                for h in range(HG):
                    c0 = 32 * (gk * HG + h) + V_AT - HV * (gk % SET)
                    last = mm(psY[32 * h:32 * h + 32, kb * 128:T],
                              Va[bpar][:, kb].rearrange("p h c -> p (h c)")[:, c0:c0 + 32],
                              p_view(P[gk % 2], h, kb), kb == 0 and gk % SET == 0,
                              kb == NT - 1 and gk in (SET - 1, NG - 1))
                if kb == NT - 1:
                    last.then_inc(S["pv_done"], 1)

            def job(s, par, on):
                def max_rows(k):
                    G = 4 * s + k + 1
                    misc_free(pe, s, on, ("m", k))
                    wait(pe, "n_ready", G + 1)
                    for seg, t in enumerate((2, 0, 1, 3)):
                        o = psM[MAX_ROW:MAX_ROW + PARTS * HG, t * 64:(t + 1) * 64].bitcast(bf16)
                        last = pe.transpose(o, nparts[:, (k + 1) % 2, seg].rearrange("p a h -> p (a h)"),
                                            identb[:, :])
                    last.then_inc(S["m_turned"], 1)

                def turn(dst_j, name, ready, count, jb):
                    bank = bank_of(s, *jb)
                    misc_free(pe, s, on, jb)
                    wait(pe, ready, count)
                    for t in range(NT):
                        last = pe.transpose(bank[:, t * 128:(t + 1) * 128], xn[:, dst_j, t], ident[:, :])
                    last.then_inc(S[name], 1)

                def project(j, name, jb):
                    misc_free(pe, s, on, jb)
                    wait(pe, "qk_split", 2)
                    wait(pe, "h_low", s + 2)
                    product(psM[:, :], QK_high[:, j], QK_low[:, j], "h").then_inc(S[name], 1)

                def turn_y(n):
                    misc_free(pe, s, on, ("y", n))
                    wait(pe, "y_copied", SETS * s)
                    for t in range(YT):
                        for m in range(SETS):
                            c0 = (t * SETS + m) * 128
                            t0 = (n * YT + t) * 128
                            last = pe.transpose(bank_of(s, "y", n)[:, c0:c0 + 128], Y[1 - par][:, m, t0:t0 + 128],
                                                ident[:, :])
                    last.then_inc(S["y_turned"], 1)

                def gate_state(weights, name, first):
                    misc_free(pe, s, on, (name, 0))
                    wait(pe, "w_split", 1)
                    wait(pe, "s_low", s)
                    return product(bank_of(s, name), *gate_halves("u" + weights), "s", first, not first)

                def gate_input(weights, name, first):
                    misc_free(pe, s, on, (name, 0))
                    wait(pe, "w_split", 1)
                    wait(pe, "h2_low", s)
                    return product(bank_of(s, name), *gate_halves("w" + weights), "h2", first, not first)

                def gate(weights, name):
                    if s < B:
                        gate_input(weights, name, True)
                        gate_state(weights, name, False).then_inc(S[name + "_made"], 1)
                    else:
                        gate_input(weights, name, False).then_inc(S[name + "_made"], 1)

                for k in range(NG):
                    for i in range(B_ITEMS):
                        if on["b"]:
                            if k == 0 and i == 0 and isinstance(s, int) and s == 0:
                                pe.wait_ge(S["sel_in"], 32)
                                pe.wait_ge(S["gate_done"], 4)
                            if i == 0:
                                wait(pe, "m_copied", NG * s + k + 1)
                            scores(4 * s + k, k, par, i)
                        if on["a"][k]:
                            G = 4 * s + k + LEAD
                            if k == 2 and i == 0:
                                wait(pe, "stacks_in", LOADS * (s + 2))
                            scores_max(G, (k + LEAD) % 4, par if k < 2 else 1 - par, 2 * i)
                        if i < NT:
                            if k == 0 and on["post"]:
                                values(4 * s - 1, 3, 1 - par, i)
                            if k > 0 and on["b"]:
                                values(4 * s + k - 1, k - 1, par, i)
                        if on["a"][k] and (k, i) not in LATE_SECOND:
                            scores_max(G, (k + LEAD) % 4, par if k < 2 else 1 - par, 2 * i + 1)
                        if (k, i) == (0, 3) and on["post2"]:
                            misc_free(pe, s, on, ("z", 0))
                            for t in range(NT):
                                last = mm(bank_of(s, "z")[:, t * 128:(t + 1) * 128], h2T[:, t * 128:(t + 1) * 128],
                                          w("woT"))
                            last.then_inc(S["z_made"], 1)
                        if (k, i) == (0, 4) and on["v"]:
                            misc_free(pe, s, on, ("v", 0))
                            wait(pe, "h_copied", s + 2)
                            for t in range(NT):
                                last = mm(psM[:, t * 128:(t + 1) * 128], hT[:, t * 128:(t + 1) * 128], WV[:, :])
                            last.then_inc(S["v_made"], 1)
                        if i == M_AT[k] and on["m"][k]:
                            max_rows(k)
                        if on["post"] and (k, i) in ((1, 0), (1, 1)):
                            turn_y(i)
                        if (k, i) == (1, 3) and on["pre"]:
                            turn(0, "h_turned", "xn_done", s + 3, ("h", 0))
                        if (k, i) == Q_STEP[s == -1] and on["pre"]:
                            project(0, "q_made", ("q", 0))
                        if (k, i) == K_STEP[s == -1] and on["pre"]:
                            project(1, "k_made", ("k", 0))
                        if (k, i) == (2, 4) and s == B:
                            for weights, name in (("fT", "f"), ("iT", "i"), ("cT", "g")):
                                gate_state(weights, name, True)
                        if (k, i) == (2, 4) and on["post"]:
                            turn(1, "h2_turned", "xn2_done", s, ("h2", 0))
                        if (k, i) == (3, 1) and on["post"]:
                            gate("fT", "f")
                        if (k, i) == (3, 3) and on["post"]:
                            gate("iT", "i")
                        if (k, i) == (3, 4) and on["post"]:
                            gate("cT", "g")
                        if on["a"][k] and (k, i) in LATE_SECOND:
                            scores_max(G, (k + LEAD) % 4, par if k < 2 else 1 - par, 2 * i + 1)

            slots(pe, job)
            pe.wait_ge(S["bo_in"], 16)
            pe.wait_ge(S["y_scaled"], NY * B)
            for t in range(NT):
                mm(psB[:, 1, t * 128:(t + 1) * 128], onesR[:, :], boR[:, :], t == 0, False)
            pe.wait_ge(S["s_done"], B)
            for t in range(NT):
                last = mm(psB[:, 1, t * 128:(t + 1) * 128], sT[:, t * 128:(t + 1) * 128], w("uoT"), False, t == NT - 1)
            last.then_inc(S["cu_made"], 1)


def kernel(**inputs):
    import concourse.bacc as bacc
    from concourse.bass_utils import run_bass_kernel_spmd

    a = {k.replace("L0_", "").replace("attn_", "").replace("ffn_", ""): np.asarray(v) for k, v in inputs.items()}
    col = {"W_uk": a["W_uk"], "W_uv": a["W_uv"], "W_oT": a["W_o"].T, "wmod": a["wmod"], "cT": a["c"].T}
    for n in ("wf", "wi", "wc", "wo", "uf", "ui", "uc", "uo"):
        col[n + "T"] = a[n].T
    for n in ("bf", "bi", "bc", "in_c"):
        col[n] = a[n][:, None]
    arrays = {
        "x": np.ascontiguousarray(a["x"]),
        "w64": np.ascontiguousarray(np.concatenate([a["W_dq"], a["W_uq"].T, a["W_dkv"]], axis=1)),
        "w128": np.ascontiguousarray(np.concatenate([col[n] for n in W128], axis=1)),
        "bo": np.ascontiguousarray(a["bo"][None, :]),
    }
    heads = np.concatenate([np.arange(0, NH, 2), np.arange(1, NH, 2)])
    own = (np.arange(PARTS * HG)[:, None] % HG) == (heads[None, :] % HG)
    arrays["sel"] = np.repeat(own[:, :, None], T, axis=2).astype(np.uint16) * ONE_BF16
    nc = bacc.Bacc("TRN2", target_bir_lowering=False, num_devices=1)
    f32 = mybir.dt.float32
    aps = [nc.dram_tensor(k, v.shape, mybir.dt.from_np(v.dtype), kind="ExternalInput").ap()
           for k, v in arrays.items()]
    scratch = nc.dram_tensor("scratch", [2, PARTS, 2, HS, NH // 2, T], mybir.dt.bfloat16, kind="Internal").ap()
    out = nc.dram_tensor("out", [B, T, C], f32, kind="ExternalOutput").ap()
    build(nc, *aps, scratch, out)
    r = run_bass_kernel_spmd(nc, [arrays], core_ids=[0])
    return r.results[0]["out"]
```
